# Optimizing a Trainium2 kernel written in Bass

```python
import numpy as np
import jax
import jax.numpy as jnp

def _softmax(x, axis=-1):
    return jax.nn.softmax(x, axis=axis)

def _gelu(x):
    return jax.nn.gelu(x, approximate=True)

def _silu(x):
    return jax.nn.silu(x)

def _sigmoid(x):
    return jax.nn.sigmoid(x)

def _layernorm(x, axis=-1, eps=1e-05):
    m = jnp.mean(x, axis=axis, keepdims=True)
    v = jnp.var(x, axis=axis, keepdims=True)
    return (x - m) / jnp.sqrt(v + eps)

def _scatter_add(tgt, idx, src, axis=0):
    return tgt.at[idx].add(src)

def _segment_sum(src, seg, n):
    return jax.ops.segment_sum(src, seg, n)
kernel_name = 'mk_prb_d1_jaxref_r8_bfc176'

def setup_inputs(seed: int=0):
    np.random.seed(seed)
    _w = jnp.asarray

    def _L0_attn_setup():
        import jax, jax.numpy as jnp
        import numpy as np
        BATCH, SEQ, DMODEL, DHID = (4, 512, 128, 128)
        R_MIN, R_MAX = (0.9, 0.99)
        MAX_PHASE = np.pi / 50
        EPS = 1e-05
        key = jax.random.key(seed)
        ks = jax.random.split(key, 8)
        u1 = jax.random.uniform(ks[0], (DHID,)) * (1 - EPS) + EPS
        mag_sq = u1 * (R_MAX ** 2 - R_MIN ** 2) + R_MIN ** 2
        nu_log = jnp.log(-0.5 * jnp.log(mag_sq + EPS))
        u2 = jax.random.uniform(ks[1], (DHID,)) * (1 - EPS) + EPS
        theta_log = jnp.log(MAX_PHASE * u2)
        B_re = jax.random.normal(ks[2], (DHID, DMODEL)) / np.sqrt(2 * DMODEL)
        B_im = jax.random.normal(ks[3], (DHID, DMODEL)) / np.sqrt(2 * DMODEL)
        C_re = jax.random.normal(ks[4], (DMODEL, DHID)) / np.sqrt(DHID)
        C_im = jax.random.normal(ks[5], (DMODEL, DHID)) / np.sqrt(DHID)
        D_skip = jax.random.normal(ks[6], (DMODEL,))
        inputs = jax.random.normal(ks[7], (BATCH, SEQ, DMODEL), dtype=jnp.float32)
        return {'inputs': inputs, 'nu_log': nu_log, 'theta_log': theta_log, 'B_re': B_re, 'B_im': B_im, 'C_re': C_re, 'C_im': C_im, 'D_skip': D_skip}
    _L0_attn_in = _L0_attn_setup()

    def _L0_ffn_setup():
        import jax, jax.numpy as jnp
        import numpy as np
        H = 128
        I = 88
        E = 64
        TOP_K = 8
        NG = 8
        TOPK_GROUP = 4
        N_SHARED = 2
        ROUTED_SCALE = 2.5
        S_I = I * N_SHARED

        def _route(x, gate_w, gate_bias):
            T = x.shape[0]
            logits = x @ gate_w.T
            scores = jax.nn.sigmoid(logits)
            scores_for_choice = scores + gate_bias[None, :]
            grp = scores_for_choice.reshape(T, NG, E // NG)
            group_scores = jnp.sum(jax.lax.top_k(grp, 2)[0], axis=-1)
            _, gidx = jax.lax.top_k(group_scores, TOPK_GROUP)
            gmask = jnp.zeros((T, NG), dtype=scores.dtype).at[jnp.arange(T)[:, None], gidx].set(1.0)
            emask = jnp.repeat(gmask, E // NG, axis=1)
            masked = jnp.where(emask > 0, scores_for_choice, 0.0)
            _, topk_idx = jax.lax.top_k(masked, TOP_K)
            topk_w = jnp.take_along_axis(scores, topk_idx, axis=1)
            topk_w = topk_w / (jnp.sum(topk_w, axis=-1, keepdims=True) + 1e-20)
            topk_w = topk_w * ROUTED_SCALE
            rw = jnp.zeros((T, E), dtype=scores.dtype).at[jnp.arange(T)[:, None], topk_idx].add(topk_w)
            return rw

        def _mlp(x, gw, uw, dw):
            return jax.nn.silu(x @ gw.T) * (x @ uw.T) @ dw.T
        key = jax.random.key(seed)
        ks = jax.random.split(key, 10)
        sc = 0.02
        return {'hidden_states': jax.random.normal(ks[0], (1, 128, H), dtype=jnp.float32), 'gate_w': sc * jax.random.normal(ks[1], (E, H), dtype=jnp.float32), 'gate_bias': sc * jax.random.normal(ks[2], (E,), dtype=jnp.float32), 'Wg': sc * jax.random.normal(ks[3], (E, I, H), dtype=jnp.float32), 'Wu': sc * jax.random.normal(ks[4], (E, I, H), dtype=jnp.float32), 'Wd': sc * jax.random.normal(ks[5], (E, H, I), dtype=jnp.float32), 'Sg': sc * jax.random.normal(ks[6], (S_I, H), dtype=jnp.float32), 'Su': sc * jax.random.normal(ks[7], (S_I, H), dtype=jnp.float32), 'Sd': sc * jax.random.normal(ks[8], (H, S_I), dtype=jnp.float32)}
    _L0_ffn_in = _L0_ffn_setup()
    _d = {'L0_attn_inputs': _L0_attn_in['inputs'], 'L0_attn_nu_log': _L0_attn_in['nu_log'], 'L0_attn_theta_log': _L0_attn_in['theta_log'], 'L0_attn_B_re': _L0_attn_in['B_re'], 'L0_attn_B_im': _L0_attn_in['B_im'], 'L0_attn_C_re': _L0_attn_in['C_re'], 'L0_attn_C_im': _L0_attn_in['C_im'], 'L0_attn_D_skip': _L0_attn_in['D_skip'], 'L0_ffn_gate_w': _L0_ffn_in['gate_w'], 'L0_ffn_gate_bias': _L0_ffn_in['gate_bias'], 'L0_ffn_Wg': _L0_ffn_in['Wg'], 'L0_ffn_Wu': _L0_ffn_in['Wu'], 'L0_ffn_Wd': _L0_ffn_in['Wd'], 'L0_ffn_Sg': _L0_ffn_in['Sg'], 'L0_ffn_Su': _L0_ffn_in['Su'], 'L0_ffn_Sd': _L0_ffn_in['Sd']}
    _x0 = _d['L0_attn_inputs']
    _d['L0_attn_inputs'] = jax.random.normal(jax.random.fold_in(jax.random.key(seed), 1), (16, 256, 128), dtype=_x0.dtype)
    del _x0
    return _d

def reference(L0_attn_inputs, L0_attn_nu_log, L0_attn_theta_log, L0_attn_B_re, L0_attn_B_im, L0_attn_C_re, L0_attn_C_im, L0_attn_D_skip, L0_ffn_gate_w, L0_ffn_gate_bias, L0_ffn_Wg, L0_ffn_Wu, L0_ffn_Wd, L0_ffn_Sg, L0_ffn_Su, L0_ffn_Sd):

    def _L0_attn_ref(inputs, nu_log, theta_log, B_re, B_im, C_re, C_im, D_skip):
        import jax, jax.numpy as jnp
        import numpy as np
        BATCH, SEQ, DMODEL, DHID = (4, 512, 128, 128)
        R_MIN, R_MAX = (0.9, 0.99)
        MAX_PHASE = np.pi / 50
        EPS = 1e-05
        nu = jnp.exp(nu_log)
        theta = jnp.exp(theta_log)
        diag_lambda = jnp.exp(-nu + 1j * theta)
        gamma_log = 0.5 * jnp.log(1 - jnp.exp(-2 * jnp.exp(nu_log)) + EPS)
        B_norm = (B_re + 1j * B_im) * jnp.exp(gamma_log)[:, None]
        inputs_c = inputs.astype(jnp.complex64)
        Bu = jnp.einsum('hd,btd->bth', B_norm, inputs_c)

        def step(h, bu_t):
            h = diag_lambda * h + bu_t
            return (h, h)
        h0 = jnp.zeros((inputs.shape[0], diag_lambda.shape[0]), dtype=Bu.dtype)
        _, hs = jax.lax.scan(step, h0, jnp.swapaxes(Bu, 0, 1))
        hs = jnp.swapaxes(hs, 0, 1)
        C_complex = C_re + 1j * C_im
        out = jnp.einsum('bth,dh->btd', hs, C_complex).real + inputs * D_skip
        return out.astype(jnp.float32)

    def _L0_ffn_ref(hidden_states, gate_w, gate_bias, Wg, Wu, Wd, Sg, Su, Sd):
        import jax, jax.numpy as jnp
        import numpy as np
        H = 128
        I = 88
        E = 64
        TOP_K = 8
        NG = 8
        TOPK_GROUP = 4
        N_SHARED = 2
        ROUTED_SCALE = 2.5
        S_I = I * N_SHARED

        def _route(x, gate_w, gate_bias):
            T = x.shape[0]
            logits = x @ gate_w.T
            scores = jax.nn.sigmoid(logits)
            scores_for_choice = scores + gate_bias[None, :]
            grp = scores_for_choice.reshape(T, NG, E // NG)
            group_scores = jnp.sum(jax.lax.top_k(grp, 2)[0], axis=-1)
            _, gidx = jax.lax.top_k(group_scores, TOPK_GROUP)
            gmask = jnp.zeros((T, NG), dtype=scores.dtype).at[jnp.arange(T)[:, None], gidx].set(1.0)
            emask = jnp.repeat(gmask, E // NG, axis=1)
            masked = jnp.where(emask > 0, scores_for_choice, 0.0)
            _, topk_idx = jax.lax.top_k(masked, TOP_K)
            topk_w = jnp.take_along_axis(scores, topk_idx, axis=1)
            topk_w = topk_w / (jnp.sum(topk_w, axis=-1, keepdims=True) + 1e-20)
            topk_w = topk_w * ROUTED_SCALE
            rw = jnp.zeros((T, E), dtype=scores.dtype).at[jnp.arange(T)[:, None], topk_idx].add(topk_w)
            return rw

        def _mlp(x, gw, uw, dw):
            return jax.nn.silu(x @ gw.T) * (x @ uw.T) @ dw.T
        B, S, _ = hidden_states.shape
        x = hidden_states.reshape(B * S, H)
        rw = _route(x, gate_w, gate_bias)
        expert_out = jax.vmap(lambda gw_, uw_, dw_: _mlp(x, gw_, uw_, dw_))(Wg, Wu, Wd)
        routed = jnp.einsum('eth,te->th', expert_out, rw)
        shared = _mlp(x, Sg, Su, Sd)
        out = (routed + shared).reshape(B, S, H)
        return out
    x = L0_attn_inputs
    xn = _layernorm(x, axis=-1)
    x = x + _L0_attn_ref(xn, L0_attn_nu_log, L0_attn_theta_log, L0_attn_B_re, L0_attn_B_im, L0_attn_C_re, L0_attn_C_im, L0_attn_D_skip) + _L0_ffn_ref(xn, L0_ffn_gate_w, L0_ffn_gate_bias, L0_ffn_Wg, L0_ffn_Wu, L0_ffn_Wd, L0_ffn_Sg, L0_ffn_Su, L0_ffn_Sd)
    return x

_drawn_inputs = setup_inputs


def setup_inputs(seed=0):
    import zlib

    import numpy as np

    out = dict(_drawn_inputs(seed))
    spreads = {}
    factors = {'L0_ffn_gate_w': 8.0,
     'L0_ffn_gate_bias': 8.0,
     'L0_ffn_Wg': 8.0,
     'L0_ffn_Wu': 8.0,
     'L0_ffn_Wd': 8.0,
     'L0_ffn_Sg': 8.0,
     'L0_ffn_Su': 8.0,
     'L0_ffn_Sd': 8.0}
    for name, (base, spread) in spreads.items():
        noise = np.random.default_rng([zlib.crc32(name.encode()), seed]).standard_normal(out[name].shape)
        drawn = base * np.exp(spread * noise) if base else spread * noise
        out[name] = jnp.asarray(drawn.astype(out[name].dtype))
    for name, factor in factors.items():
        out[name] = (out[name] * factor).astype(out[name].dtype)
    return out
```

```python
from contextlib import ExitStack

import concourse.bass as bass
from concourse import mybir

F32 = mybir.dt.float32
F32R = mybir.dt.float32r
ALU = mybir.AluOpType
ACT = mybir.ActivationFunctionType
AX = mybir.AxisListType

P = 128
PI = 3.14159265358979
TWO_PI_A = 6.28125
TWO_PI_B = 2 * PI - TWO_PI_A
ROUND = 12582912.0
GONE = -3.0e38
LN_EPS = 1e-05
LRU_EPS = 1e-05
WEIGHT_EPS = 1e-20
ROUTED_SCALE = 2.5
TOP_GROUPS = 4

DVE_STEPS = ["stats", "mean_var", "xn", "turned_in", "scan",
             "choice", "pair_max", "quad_max", "quad_second", "group_max", "group_second", "group_score",
             "beats", "ties", "order", "rank", "group_mask", "masked", "masked_zero", "top8", "struck",
             "chosen", "chosen_sum", "sum_eps", "sum_inv", "weight", "weight_T", "x_lo"]
ACT_STEPS = ["x_T", "scores", "x_hi"]
POOL_STEPS = ["var_eps", "rstd", "turned", "back_products", "state", "skip"]
PE_STEPS = ["x_turn", "logits", "drive", "weight_turn", "lru_out"]
POOL_SETUP = ["consts", "masks", "rates", "exponents", "powers", "one_e2", "one_e2_eps", "gamma"]
DVE_SETUP = ["angle", "turns", "whole_turns", "less_a", "less_b", "clamped", "size", "tables", "lru_T", "gate_T",
             "shared_lo"]
ACT_SETUP = ["sin_cos", "shared_hi"]
PE_SETUP = ["lru_turn", "shared_turn", "down_turn"]


def after(eng, semaphore, steps, name, n=0):
    eng.wait_ge(semaphore, n * len(steps) + steps.index(name) + 1)


def build(nc, x, nu_log, theta_log, B_re, B_im, C_re, C_im, D_skip, gate_w, gate_bias,
          Wg, Wu, Wd, Sg, Su, Sd, out):
    BATCH, SEQ, D = x.shape
    E, I, _ = Wg.shape
    NG = 8
    PG = E // NG
    T = 512
    SUB = T // P
    NT = BATCH * SEQ // T
    NSEQ = T // SEQ
    R = P // E
    J = I // R
    SC = 2
    SH = Sg.shape[0] // SC
    U = J + SC
    LAG = 3
    HEAD = 5
    BUF = 2
    PARTS = 4
    assert U % BUF == 0 and D == P and R * E == P and HEAD > LAG

    x_tiles = x.rearrange("b s d -> (b s) d").rearrange("(t s p) d -> t p s d", p=P, s=SUB)
    out_tiles = out.rearrange("b s d -> (b s) d").rearrange("(t s p) d -> t p s d", p=P, s=SUB)

    ctx = ExitStack()
    with ctx:
        def sb(name, shape, dt=F32):
            return ctx.enter_context(nc.sbuf_tensor(name, shape, dt))

        def pb(name):
            return ctx.enter_context(nc.psum_tensor(name, [P, 512], F32))

        def sem(name):
            return ctx.enter_context(nc.semaphore(name))

        wg = [sb(f"wg_{h}", [P, J * P], F32R) for h in ("hi", "lo")]
        wu = [sb(f"wu_{h}", [P, J * P], F32R) for h in ("hi", "lo")]
        wd = [sb(f"wd_{h}", [P, J * D], F32R) for h in ("hi", "lo")]
        sg = [sb(f"sg_{h}", [P, SC * SH], F32R) for h in ("hi", "lo")]
        su = [sb(f"su_{h}", [P, SC * SH], F32R) for h in ("hi", "lo")]
        sd = [sb(f"sd_{h}", [SH, SC * D], F32R) for h in ("hi", "lo")]
        gate_T = sb("gate_T", [P, E])
        lru_T = sb("lru_T", [P, 4 * P])
        bias = sb("bias", [P, E])
        ident = sb("ident", [P, P])
        before = sb("before", [P, NG, NG])
        cols = sb("cols", [P, 16])
        cos_t = sb("cos_t", [P, SEQ])
        sin_t = sb("sin_t", [P, SEQ])
        gcos_t = sb("gcos_t", [P, SEQ])
        gsin_t = sb("gsin_t", [P, SEQ])
        decay = sb("decay", [P, SEQ])
        minus_half = sb("minus_half", [P, SUB])
        eps = sb("eps", [P, SUB])
        x_in = sb("x_in", [P, SUB, D])
        x_res = sb("x_res", [P, SUB, D])
        x_T = sb("x_T", [P, T])
        x_hi = sb("x_hi", [P, T], F32R)
        x_lo = sb("x_lo", [P, T], F32R)
        weight_T = sb("weight_T", [P, T])
        skip = sb("skip", [P, T])
        h_re = sb("h_re", [P, T])
        h_im = sb("h_im", [P, T])
        lru = sb("lru", [P, 4, T])
        small = sb("small", [P, 64])
        route = sb("route", [P, 7 * SUB * E])
        work = sb("work", [P, 3 * BUF * T])
        act_g = work[:, 0:BUF * T].rearrange("p (b t) -> p b t", b=BUF)
        up_w = work[:, BUF * T:2 * BUF * T].rearrange("p (b t) -> p b t", b=BUF)
        hid = work[:, 2 * BUF * T:3 * BUF * T].rearrange("p (b t) -> p b t", b=BUF)
        hid_hi = sb("hid_hi", [P, PARTS, T], F32R)
        hid_lo = sb("hid_lo", [P, PARTS, T], F32R)

        stats = small[:, 0:24].rearrange("p (s k) -> p s k", k=6)
        mv = small[:, 24:32].rearrange("p (s k) -> p s k", k=2)
        var_eps, rstd, w_sum, w_sum_eps, w_inv = (small[:, 32 + SUB * k:32 + SUB * (k + 1)] for k in range(5))
        y_T = lru[:, 0, :]

        (NU_LOG, THETA_LOG, DSKIP, NU, THETA, NEG_NU, DECAY, NEG_2NU, E2, ONE_E2, ONE_E2_EPS, GAMMA, BASE_E,
         HALF, HALF_PI) = range(15)

        def col(k):
            return cols[:, k:k + 1]

        def part(k):
            return route[:, k * SUB * E:(k + 1) * SUB * E]

        NSG = SUB * NG
        scores, choice = part(0), part(1)
        hi4, lo4 = (part(2)[:, k * NSG * 4:(k + 1) * NSG * 4].rearrange("p (g k) -> p g k", k=4) for k in range(2))
        hi2, mid2, low2, second2 = (part(3)[:, k * NSG * 2:(k + 1) * NSG * 2].rearrange("p (g k) -> p g k", k=2)
                                    for k in range(4))
        best, mid1, low1, second, score, rank, group_mask = (part(4)[:, k * NSG:(k + 1) * NSG] for k in range(7))
        top8 = part(4)[:, 7 * NSG:8 * NSG].rearrange("p (s k) -> p s k", k=8)
        beats, ties = (part(k).rearrange("p (g h) -> p g h", h=NG) for k in (5, 6))
        masked, masked_zero, struck, chosen = part(5), part(6), part(5), part(6)
        weight = route[:, 2 * SUB * E:4 * SUB * E].rearrange("p (s e r) -> p s e r", s=SUB, r=R)

        p_g = [pb(f"p_g{i}") for i in range(2)]
        p_u = [pb(f"p_u{i}") for i in range(2)]
        p_y = pb("p_y")
        p_a = pb("p_a")
        p_b = pb("p_b")
        p_c = pb("p_c")

        raw_lru = skip[:, :]
        raw_gate = route[0:E, 0:D]
        raw_sg, raw_su = (route[0:SH, D + k * SC * D:D + (k + 1) * SC * D].rearrange("p (c d) -> p c d", c=SC)
                          for k in range(2))
        raw_sd = route[:, 5 * D:5 * D + SC * SH]
        GATE_AT, SG_AT, SU_AT = 0, E, E + SC * SH
        STAGES = 3
        stage = [work[:, k * BUF * T:(k + 1) * BUF * T] for k in range(STAGES)]
        PIECE = BUF * T // P
        ROWS = 16
        GROUP = 4
        turn_banks = p_g + p_u
        pieces = [(m, a, min(a + PIECE, J)) for m in range(2) for a in range(0, J, PIECE)]
        pieces += [(2, a, a + ROWS) for a in range(0, D, ROWS)]
        groups = [(m, a) for m in range(2) for a in range(0, J, GROUP)]
        downs = [(i, a) for i, (m, a, _) in enumerate(pieces) if m == 2]
        N_PARTS = len(groups) + len(downs)
        arrivals, loaded_at = [0] * STAGES, []
        for i, (m, _, _) in enumerate(pieces):
            arrivals[i % STAGES] += 16 * (R if m == 2 else 1)
            loaded_at.append(arrivals[i % STAGES])

        vectors_in = sem("vectors_in")
        raw_in = sem("raw_in")
        stage_in = [sem(f"stage_in{k}") for k in range(STAGES)]
        x_loaded = sem("x_loaded")
        res_loaded = sem("res_loaded")
        stored = sem("stored")
        pool_setup, dve_setup, act_setup, pe_setup = (sem(f"{e}_setup") for e in ("pool", "dve", "act", "pe"))
        pool_step, dve_step, act_step, pe_step = (sem(f"{e}_step") for e in ("pool", "dve", "act", "pe"))
        w_turned, w_hi, w_lo = sem("w_turned"), sem("w_hi"), sem("w_lo")
        g_ready, u_ready, silu_ready, up_ready, hid_ready, hi_ready, lo_ready, y_done = (
            sem(s) for s in ("g_ready", "u_ready", "silu_ready", "up_ready", "hid_ready", "hi_ready", "lo_ready",
                             "y_done"))
        y_moved, y_turned, out_ready = sem("y_moved"), sem("y_turned"), sem("out_ready")

        def rows(j):
            return P if j < J else SH

        def parts_free(eng, n, j):
            if j >= PARTS:
                eng.wait_ge(y_done, U * n + j - PARTS + 1)
            elif not (isinstance(n, int) and n == 0):
                last = max(i for i in range(U) if i % PARTS == j)
                eng.wait_ge(y_done, U * (n - 1) + last + 1)

        def first(n):
            return isinstance(n, int) and n == 0

        block = ctx.enter_context(nc.Block())

        @block.sync
        def _(sp):
            sp.dma_start(x_in[:, :, :], x_tiles[0]).then_inc(x_loaded, 16)
            for k, v in ((NU_LOG, nu_log), (THETA_LOG, theta_log), (DSKIP, D_skip)):
                sp.dma_start(col(k), v.rearrange("(p o) -> p o", o=1)).then_inc(vectors_in, 16)
            for k, m in enumerate((B_re, B_im, C_re, C_im)):
                sp.dma_start(raw_lru[:, k * P:(k + 1) * P], m).then_inc(raw_in, 16)
            sp.dma_start(raw_gate, gate_w).then_inc(raw_in, 16)
            sp.dma_start(raw_sg, Sg.rearrange("(c p) d -> p c d", c=SC)).then_inc(raw_in, 16)
            sp.dma_start(raw_su, Su.rearrange("(c p) d -> p c d", c=SC)).then_inc(raw_in, 16)
            sp.dma_start(raw_sd, Sd).then_inc(raw_in, 16)
            sp.dma_start(bias[:, :], gate_bias.partition_broadcast(P)).then_inc(raw_in, 16)
            wide = [w.rearrange("e (r j) d -> (e r) j d", r=R) for w in (Wg, Wu)]
            for i, (m, a, b) in enumerate(pieces):
                if i >= STAGES:
                    lm, la, lb = pieces[i - STAGES]
                    if lm < 2:
                        sp.wait_ge(w_turned, lm * J // GROUP + (lb + GROUP - 1) // GROUP)
                    else:
                        sp.wait_ge(w_lo, len(groups) + la // ROWS + 1)
                s = stage[i % STAGES]
                if m < 2:
                    sp.dma_start(s[:, 0:(b - a) * D].rearrange("p (j d) -> p j d", d=D),
                                 wide[m][:, a:b, :]).then_inc(stage_in[i % STAGES], 16)
                else:
                    for r in range(R):
                        sp.dma_start(s[r::R, 0:ROWS * J].rearrange("p (d j) -> p d j", j=J),
                                     Wd[:, a:b, r * J:(r + 1) * J]).then_inc(stage_in[i % STAGES], 16)
            sp.dma_start(x_res[:, :, :], x_tiles[0]).then_inc(res_loaded, 16)

            def store(n):
                sp.wait_ge(out_ready, n + 1)
                sp.dma_start(out_tiles[n], x_res[:, :, :]).then_inc(stored, 16)

            with sp.Fori(0, NT - 1) as t:
                after(sp, pe_step, PE_STEPS, "x_turn", t)
                sp.dma_start(x_in[:, :, :], x_tiles[t + 1]).then_inc(x_loaded, 16)
                store(t)
                sp.wait_ge(stored, 16 * t + 16)
                sp.dma_start(x_res[:, :, :], x_tiles[t + 1]).then_inc(res_loaded, 16)
            store(NT - 1)
            sp.wait_ge(stored, 16 * NT)

        @block.gpsimd
        def _(pool):
            pool.memset(ident[:, :], 0.0)
            pool.memset(before[:, :, :], 1.0)
            pool.memset(minus_half[:, :], -0.5)
            pool.memset(eps[:, :], LN_EPS)
            pool.memset(col(BASE_E), 2.718281828459045)
            pool.memset(col(HALF), 0.5)
            pool.memset(col(HALF_PI), PI / 2)
            pool.iota(decay[:, :], [[1, SEQ]], base=0, channel_multiplier=0,
                      allow_small_or_imprecise_dtypes=True).then_inc(pool_setup, 1)
            after(pool, pool_setup, POOL_SETUP, "consts")
            pool.affine_select(out=ident[:, :], in_=ident[:, :], compare_op=ALU.not_equal, fill=1.0,
                               base=0, pattern=[[-1, P]], channel_multiplier=1)
            pool.affine_select(out=before[:, :, :], in_=before[:, :, :], compare_op=ALU.is_gt, fill=0.0,
                               base=0, pattern=[[1, NG], [-1, NG]], channel_multiplier=0).then_inc(pool_setup, 1)
            pool.wait_ge(vectors_in, 48)
            pool.tensor_tensor(col(NU), col(BASE_E), col(NU_LOG), ALU.pow)
            pool.tensor_tensor(col(THETA), col(BASE_E), col(THETA_LOG), ALU.pow).then_inc(pool_setup, 1)
            after(pool, pool_setup, POOL_SETUP, "rates")
            pool.tensor_scalar(col(NEG_NU), col(NU), -1.0, None, ALU.mult)
            pool.tensor_scalar(col(NEG_2NU), col(NU), -2.0, None, ALU.mult).then_inc(pool_setup, 1)
            after(pool, pool_setup, POOL_SETUP, "exponents")
            pool.tensor_tensor(col(DECAY), col(BASE_E), col(NEG_NU), ALU.pow)
            pool.tensor_tensor(col(E2), col(BASE_E), col(NEG_2NU), ALU.pow).then_inc(pool_setup, 1)
            after(pool, pool_setup, POOL_SETUP, "powers")
            pool.tensor_scalar(col(ONE_E2), col(E2), -1.0, 1.0, ALU.mult, ALU.add).then_inc(pool_setup, 1)
            after(pool, pool_setup, POOL_SETUP, "one_e2")
            pool.tensor_scalar(col(ONE_E2_EPS), col(ONE_E2), LRU_EPS, None, ALU.add).then_inc(pool_setup, 1)
            after(pool, pool_setup, POOL_SETUP, "one_e2_eps")
            pool.tensor_tensor(col(GAMMA), col(ONE_E2_EPS), col(HALF), ALU.pow).then_inc(pool_setup, 1)

            def norm_scale(n):
                after(pool, dve_step, DVE_STEPS, "mean_var", n)
                pool.tensor_tensor(var_eps, mv[:, :, 1], eps[:, :], ALU.add).then_inc(pool_step, 1)
                after(pool, pool_step, POOL_STEPS, "var_eps", n)
                pool.tensor_tensor(rstd, var_eps, minus_half[:, :], ALU.pow).then_inc(pool_step, 1)

            def turned(n):
                after(pool, dve_step, DVE_STEPS, "turned_in", n)
                pool.tensor_tensor(lru[:, 0, :], lru[:, 0, :], lru[:, 1, :], ALU.add)
                pool.tensor_tensor(lru[:, 2, :], lru[:, 2, :], lru[:, 3, :], ALU.subtract).then_inc(pool_step, 1)

            def time(table):
                return table[:, :].unsqueeze(1).to_broadcast([P, NSEQ, SEQ])

            def by_time(a):
                return a.rearrange("p (s t) -> p s t", t=SEQ)

            def turn_back(n):
                after(pool, dve_step, DVE_STEPS, "scan", n)
                if not first(n):
                    after(pool, pe_step, PE_STEPS, "lru_out", n - 1)
                pool.tensor_tensor(by_time(h_re[:, :]), by_time(lru[:, 1, :]), time(cos_t), ALU.mult)
                pool.tensor_tensor(by_time(lru[:, 0, :]), by_time(lru[:, 3, :]), time(sin_t), ALU.mult)
                pool.tensor_tensor(by_time(h_im[:, :]), by_time(lru[:, 1, :]), time(sin_t), ALU.mult)
                pool.tensor_tensor(by_time(lru[:, 2, :]), by_time(lru[:, 3, :]), time(cos_t),
                                   ALU.mult).then_inc(pool_step, 1)

            def state(n):
                after(pool, pool_step, POOL_STEPS, "back_products", n)
                pool.tensor_tensor(h_re[:, :], h_re[:, :], lru[:, 0, :], ALU.subtract)
                pool.tensor_tensor(h_im[:, :], h_im[:, :], lru[:, 2, :], ALU.add).then_inc(pool_step, 1)

            def skipped(n):
                after(pool, act_step, ACT_STEPS, "x_T", n)
                if first(n):
                    after(pool, pe_setup, PE_SETUP, "lru_turn")
                else:
                    pool.wait_ge(y_moved, n)
                pool.tensor_tensor(skip[:, :], x_T[:, :], col(DSKIP).to_broadcast([P, T]), ALU.mult).then_inc(pool_step, 1)

            def lo(n, j):
                k, m = U * n + j, rows(j)
                pool.wait_ge(hi_ready, k + 1)
                pool.tensor_tensor(hid_lo[0:m, j % PARTS, :], hid[0:m, j % BUF, :],
                                   hid_hi[0:m, j % PARTS, :].bitcast(F32), ALU.subtract).then_inc(lo_ready, 1)

            prepare = {10: norm_scale, 22: turned, 25: turn_back, 28: state}

            def head(n):
                for j in range(HEAD):
                    lo(n, j)
                    if j == 2:
                        skipped(n)

            for step in prepare.values():
                step(0)
            head(0)
            with pool.Fori(0, NT - 1) as t:
                for j in range(HEAD, U):
                    lo(t, j)
                    if j in prepare:
                        prepare[j](t + 1)
                head(t + 1)
            for j in range(HEAD, U):
                lo(NT - 1, j)

        @block.scalar
        def _(act):
            after(act, dve_setup, DVE_SETUP, "size")
            act.activation(sin_t[:, :], lru[:, 2, 0:SEQ], ACT.Sin)
            act.activation(cos_t[:, :], lru[:, 3, 0:SEQ], ACT.Sin, scale=-1.0, bias=col(HALF_PI)).then_inc(act_setup, 1)
            after(act, pe_setup, PE_SETUP, "down_turn")
            after(act, dve_setup, DVE_SETUP, "gate_T")
            act.copy(sg[0][:, :], p_b[:, SG_AT:SG_AT + SC * SH])
            act.copy(su[0][:, :], p_b[:, SU_AT:SU_AT + SC * SH])
            act.copy(sd[0][:, :], p_c[0:SH, 0:SC * D]).then_inc(act_setup, 1)

            def x_transposed(n):
                after(act, pe_step, PE_STEPS, "x_turn", n)
                if not first(n):
                    after(act, pool_step, POOL_STEPS, "skip", n - 1)
                    after(act, dve_step, DVE_STEPS, "x_lo", n - 1)
                act.copy(x_T[:, :], p_a[:, :]).then_inc(act_step, 1)

            def sigmoid(n):
                after(act, pe_step, PE_STEPS, "logits", n)
                if first(n):
                    after(act, pe_setup, PE_SETUP, "shared_turn")
                else:
                    after(act, dve_step, DVE_STEPS, "chosen", n - 1)
                act.activation(scores, p_b[:, 0:SUB * E], ACT.Sigmoid).then_inc(act_step, 1)

            def x_high(n):
                if not first(n):
                    act.wait_ge(u_ready, U * n)
                act.copy(x_hi[:, :], x_T[:, :]).then_inc(act_step, 1)

            def silu(n, j):
                k, m = U * n + j, rows(j)
                act.wait_ge(g_ready, k + 1)
                if not (first(n) and j < BUF):
                    act.wait_ge(hid_ready, k - BUF + 1)
                act.activation(act_g[0:m, j % BUF, :], p_g[j % 2][0:m, :], ACT.Silu).then_inc(silu_ready, 1)

            def hi(n, j):
                k, m = U * n + j, rows(j)
                act.wait_ge(hid_ready, k + 1)
                parts_free(act, n, j)
                act.copy(hid_hi[0:m, j % PARTS, :], hid[0:m, j % BUF, :]).then_inc(hi_ready, 1)

            for i, (m, a) in enumerate(groups):
                act.wait_ge(w_turned, i + 1)
                act.copy((wg, wu)[m][0][:, a * P:(a + GROUP) * P], turn_banks[i % 4][:, :]).then_inc(w_hi, 1)
            for i, a in downs:
                act.wait_ge(stage_in[i % STAGES], loaded_at[i])
                act.copy(wd[0][:, :].rearrange("p (j d) -> p d j", d=D)[:, a:a + ROWS, :],
                         stage[i % STAGES][:, 0:ROWS * J].rearrange("p (d j) -> p d j", j=J)).then_inc(w_hi, 1)
            x_transposed(0)
            sigmoid(0)
            x_high(0)
            for j in range(HEAD):
                silu(0, j)
                if j:
                    hi(0, j - 1)
            prepare = {15: x_transposed, 20: sigmoid}

            def rest(t, more):
                for j in range(HEAD, U):
                    silu(t, j)
                    hi(t, j - 1)
                    if more and j in prepare:
                        prepare[j](t + 1)

            with act.Fori(0, NT - 1) as t:
                rest(t, True)
                x_high(t + 1)
                silu(t + 1, 0)
                hi(t, U - 1)
                for j in range(1, HEAD):
                    silu(t + 1, j)
                    hi(t + 1, j - 1)
            rest(NT - 1, False)
            hi(NT - 1, U - 1)

        @block.vector
        def _(dve):
            setup_done = [0]

            def setup(ins):
                ins.then_inc(dve_setup, 1)
                setup_done[0] += 1
                dve.wait_ge(dve_setup, setup_done[0])

            angle, turns, less = (lru[:, k, 0:SEQ] for k in range(3))
            size = lru[:, 3, 0:SEQ]
            after(dve, pool_setup, POOL_SETUP, "rates")
            setup(dve.tensor_scalar(angle, decay[:, :], col(THETA), None, ALU.mult))
            setup(dve.tensor_scalar(turns, angle, 1 / (2 * PI), ROUND, ALU.mult, ALU.add))
            setup(dve.tensor_scalar(turns, turns, ROUND, None, ALU.subtract))
            setup(dve.scalar_tensor_tensor(less, turns, -TWO_PI_A, angle, ALU.mult, ALU.add))
            setup(dve.scalar_tensor_tensor(less, turns, -TWO_PI_B, less, ALU.mult, ALU.add))
            setup(dve.tensor_scalar(less, less, 3.1415925, -3.1415925, ALU.min, ALU.max))
            setup(dve.scalar_tensor_tensor(size, less, -1.0, less, ALU.mult, ALU.max))
            after(dve, pool_setup, POOL_SETUP, "gamma")
            after(dve, act_setup, ACT_SETUP, "sin_cos")
            dve.tensor_scalar(gcos_t[:, :], cos_t[:, :], col(GAMMA), None, ALU.mult)
            dve.tensor_scalar(gsin_t[:, :], sin_t[:, :], col(GAMMA), None, ALU.mult)
            setup(dve.tensor_scalar(decay[:, :], decay[:, :], 0.0, col(DECAY), ALU.mult, ALU.add))
            after(dve, pe_setup, PE_SETUP, "lru_turn")
            dve.tensor_copy(lru_T[:, 0:3 * P], p_a[:, 0:3 * P])
            setup(dve.tensor_scalar(lru_T[:, 3 * P:4 * P], p_a[:, 3 * P:4 * P], -1.0, None, ALU.mult))
            after(dve, pe_setup, PE_SETUP, "shared_turn")
            setup(dve.tensor_copy(gate_T[:, :], p_b[:, GATE_AT:GATE_AT + E]))
            after(dve, act_setup, ACT_SETUP, "shared_hi")
            dve.tensor_tensor(sg[1][:, :], p_b[:, SG_AT:SG_AT + SC * SH], sg[0][:, :].bitcast(F32), ALU.subtract)
            dve.tensor_tensor(su[1][:, :], p_b[:, SU_AT:SU_AT + SC * SH], su[0][:, :].bitcast(F32), ALU.subtract)
            setup(dve.tensor_tensor(sd[1][:, :], p_c[0:SH, 0:SC * D], sd[0][:, :].bitcast(F32), ALU.subtract))

            def split(i):
                dve.wait_ge(w_hi, i + 1)
                if i < len(groups):
                    m, a = groups[i]
                    w = (wg, wu)[m]
                    dve.tensor_tensor(w[1][:, a * P:(a + GROUP) * P], turn_banks[i % 4][:, :],
                                      w[0][:, a * P:(a + GROUP) * P].bitcast(F32), ALU.subtract).then_inc(w_lo, 1)
                else:
                    q, a = downs[i - len(groups)]
                    dve.wait_ge(stage_in[q % STAGES], loaded_at[q])
                    hi_part, lo_part = (w[:, :].rearrange("p (j d) -> p d j", d=D)[:, a:a + ROWS, :] for w in wd)
                    dve.tensor_tensor(lo_part, stage[q % STAGES][:, 0:ROWS * J].rearrange("p (d j) -> p d j", j=J),
                                      hi_part.bitcast(F32), ALU.subtract).then_inc(w_lo, 1)

            def time(table):
                return table[:, :].unsqueeze(1).to_broadcast([P, NSEQ, SEQ])

            def by_time(a):
                return a.rearrange("p (s t) -> p s t", t=SEQ)

            def step(ins, name, n):
                ins.then_inc(dve_step, 1)
                after(dve, dve_step, DVE_STEPS, name, n)

            def norm_stats(n):
                dve.wait_ge(x_loaded, 16 * n + 16)
                for s in range(SUB):
                    last = dve.bn_stats(stats[:, s, :], x_in[:, s, :])
                last.then_inc(dve_step, 1)

            def norm_aggregate(n):
                for s in range(SUB):
                    last = dve.bn_aggr(mv[:, s, :], stats[:, s, :])
                last.then_inc(dve_step, 1)

            def normalise(n):
                after(dve, pool_step, POOL_STEPS, "rstd", n)
                for s in range(SUB):
                    last = dve.tensor_scalar(x_in[:, s, :], x_in[:, s, :], mv[:, s, 0:1], rstd[:, s:s + 1],
                                             ALU.subtract, ALU.mult)
                last.then_inc(dve_step, 1)

            def turn_in(n):
                after(dve, pe_step, PE_STEPS, "drive", n)
                dve.tensor_tensor(by_time(lru[:, 0, :]), by_time(p_a[:, :]), time(gcos_t), ALU.mult)
                dve.tensor_tensor(by_time(lru[:, 1, :]), by_time(p_c[:, :]), time(gsin_t), ALU.mult)
                dve.tensor_tensor(by_time(lru[:, 2, :]), by_time(p_c[:, :]), time(gcos_t), ALU.mult)
                dve.tensor_tensor(by_time(lru[:, 3, :]), by_time(p_a[:, :]), time(gsin_t),
                                  ALU.mult).then_inc(dve_step, 1)

            def scan(n):
                after(dve, pool_step, POOL_STEPS, "turned", n)
                for k in (0, 2):
                    for s in range(NSEQ):
                        at = slice(s * SEQ, (s + 1) * SEQ)
                        last = dve.tensor_tensor_scan(lru[:, k + 1, at], decay[:, :], lru[:, k, at], 0.0,
                                                      ALU.mult, ALU.add)
                last.then_inc(dve_step, 1)

            def group_pairs(n):
                after(dve, act_step, ACT_STEPS, "scores", n)
                step(dve.tensor_tensor(choice.rearrange("p (s e) -> p s e", e=E),
                                       scores.rearrange("p (s e) -> p s e", e=E),
                                       bias[:, :].unsqueeze(1).to_broadcast([P, SUB, E]), ALU.add), "choice", n)
                c = choice.rearrange("p (g k) -> p g k", k=PG)
                dve.tensor_tensor(hi4, c[:, :, 0:4], c[:, :, 4:8], ALU.max)
                step(dve.tensor_tensor(lo4, c[:, :, 0:4], c[:, :, 4:8], ALU.min), "pair_max", n)

            def group_fours(n):
                dve.tensor_tensor(hi2, hi4[:, :, 0:2], hi4[:, :, 2:4], ALU.max)
                dve.tensor_tensor(mid2, hi4[:, :, 0:2], hi4[:, :, 2:4], ALU.min)
                step(dve.tensor_tensor(low2, lo4[:, :, 0:2], lo4[:, :, 2:4], ALU.max), "quad_max", n)
                step(dve.tensor_tensor(second2, mid2, low2, ALU.max), "quad_second", n)

            def group_scores(n):
                dve.tensor_tensor(best, hi2[:, :, 0], hi2[:, :, 1], ALU.max)
                dve.tensor_tensor(mid1, hi2[:, :, 0], hi2[:, :, 1], ALU.min)
                step(dve.tensor_tensor(low1, second2[:, :, 0], second2[:, :, 1], ALU.max), "group_max", n)
                step(dve.tensor_tensor(second, mid1, low1, ALU.max), "group_second", n)
                step(dve.tensor_tensor(score, best, second, ALU.add), "group_score", n)

            def group_rank(n):
                other = score.rearrange("p (s g) -> p s g", g=NG).unsqueeze(2).to_broadcast([P, SUB, NG, NG])
                own = score.rearrange("p (s g) -> p s g", g=NG).unsqueeze(3).to_broadcast([P, SUB, NG, NG])
                b4, t4 = (a.rearrange("p (s g) h -> p s g h", s=SUB) for a in (beats, ties))
                dve.tensor_tensor(b4, other, own, ALU.is_gt)
                step(dve.tensor_tensor(t4, other, own, ALU.is_equal), "beats", n)

            def group_ties(n):
                t3 = ties.rearrange("p (s g) h -> p s (g h)", s=SUB)
                b3 = beats.rearrange("p (s g) h -> p s (g h)", s=SUB)
                prior = before[:, :, :].rearrange("p g h -> p (g h)").unsqueeze(1).to_broadcast([P, SUB, NG * NG])
                step(dve.tensor_tensor(t3, t3, prior, ALU.mult), "ties", n)
                step(dve.tensor_tensor(b3, b3, t3, ALU.add), "order", n)
                step(dve.tensor_reduce(rank, beats, AX.X, ALU.add), "rank", n)

            def mask(n):
                step(dve.tensor_scalar(group_mask, rank, float(TOP_GROUPS), None, ALU.is_lt), "group_mask", n)
                step(dve.tensor_tensor(masked.rearrange("p (g k) -> p g k", k=PG),
                                       choice.rearrange("p (g k) -> p g k", k=PG),
                                       group_mask.unsqueeze(2).to_broadcast([P, NSG, PG]), ALU.mult), "masked", n)
                step(dve.tensor_scalar(masked_zero, masked, 0.0, None, ALU.add), "masked_zero", n)

            def choose(n):
                for s in range(SUB):
                    last = dve.max(top8[:, s, :], masked_zero[:, s * E:(s + 1) * E])
                step(last, "top8", n)

            def strike(n):
                for s in range(SUB):
                    last = dve.match_replace(struck[:, s * E:(s + 1) * E], top8[:, s, :],
                                             masked_zero[:, s * E:(s + 1) * E], GONE)
                step(last, "struck", n)
                step(dve.scalar_tensor_tensor(chosen, struck, GONE / 2, scores, ALU.is_lt, ALU.mult), "chosen", n)

            def weigh(n):
                step(dve.tensor_reduce(w_sum, chosen.rearrange("p (s e) -> p s e", e=E), AX.X, ALU.add),
                     "chosen_sum", n)
                step(dve.tensor_scalar(w_sum_eps, w_sum, WEIGHT_EPS, None, ALU.add), "sum_eps", n)
                step(dve.reciprocal(w_inv, w_sum_eps), "sum_inv", n)

            def weights(n):
                if not first(n):
                    after(dve, pe_step, PE_STEPS, "weight_turn", n - 1)
                for s in range(SUB):
                    last = dve.tensor_scalar(weight[:, s, :, :],
                                             chosen[:, s * E:(s + 1) * E].unsqueeze(2).to_broadcast([P, E, R]),
                                             w_inv[:, s:s + 1], ROUTED_SCALE, ALU.mult, ALU.mult)
                last.then_inc(dve_step, 1)

            def weight_in(n):
                after(dve, pe_step, PE_STEPS, "weight_turn", n)
                dve.tensor_copy(weight_T[:, :], p_b[:, :]).then_inc(dve_step, 1)
                after(dve, dve_step, DVE_STEPS, "weight_T", n)

            def x_low(n):
                after(dve, act_step, ACT_STEPS, "x_hi", n)
                dve.tensor_tensor(x_lo[:, :], x_T[:, :], x_hi[:, :].bitcast(F32), ALU.subtract).then_inc(dve_step, 1)

            def y_out(n):
                dve.wait_ge(y_done, U * n + U)
                after(dve, pool_step, POOL_STEPS, "skip", n)
                if not (isinstance(n, int) and n == NT - 1):
                    after(dve, pool_step, POOL_STEPS, "state", n + 1)
                dve.tensor_tensor(y_T, p_y[:, :], skip[:, :], ALU.add).then_inc(y_moved, 1)

            def add_x(n):
                dve.wait_ge(y_turned, n + 1)
                dve.wait_ge(res_loaded, 16 * n + 16)
                dve.tensor_tensor(x_res[:, :, :], p_c[:, :].rearrange("p (s d) -> p s d", s=SUB), x_res[:, :, :],
                                  ALU.add).then_inc(out_ready, 1)

            def unit(n, j):
                k, m = U * n + j, rows(j)
                dve.wait_ge(u_ready, k + 1)
                if j < J:
                    dve.tensor_tensor(up_w[0:m, j % BUF, :], p_u[j % 2][0:m, :], weight_T[0:m, :],
                                      ALU.mult).then_inc(up_ready, 1)
                    dve.wait_ge(up_ready, J * n + j + 1)
                    up = up_w[0:m, j % BUF, :]
                else:
                    up = p_u[j % 2][0:m, :]
                dve.wait_ge(silu_ready, k + 1)
                if not (first(n) and j < BUF):
                    dve.wait_ge(lo_ready, k - BUF + 1)
                dve.tensor_tensor(hid[0:m, j % BUF, :], up, act_g[0:m, j % BUF, :], ALU.mult).then_inc(hid_ready, 1)

            prepare = {8: norm_stats, 9: norm_aggregate, 12: normalise, 21: turn_in, 24: scan, 26: group_pairs, 27: group_fours,
                       28: group_scores, 29: group_rank, 30: group_ties, 31: mask, 33: choose, 34: strike,
                       36: weigh, 38: weights}

            for i in range(N_PARTS):
                split(i)
            for f in prepare.values():
                if f is norm_aggregate:
                    after(dve, dve_step, DVE_STEPS, "stats", 0)
                f(0)
            weight_in(0)
            x_low(0)
            for j in range(HEAD):
                unit(0, j)

            def rest(t, more):
                for j in range(HEAD, U):
                    if more and prepare.get(j) is norm_aggregate:
                        after(dve, dve_step, DVE_STEPS, "stats", t + 1)
                    unit(t, j)
                    if more and j in prepare:
                        prepare[j](t + 1)
                    if more and j == J:
                        weight_in(t + 1)

            with dve.Fori(0, NT - 1) as t:
                rest(t, True)
                x_low(t + 1)
                for j in range(HEAD):
                    unit(t + 1, j)
                    if j == 1:
                        y_out(t)
                    if j == 4:
                        add_x(t)
            rest(NT - 1, False)
            y_out(NT - 1)
            add_x(NT - 1)

        @block.tensor
        def _(pe):
            after(pe, pool_setup, POOL_SETUP, "masks")
            pe.wait_ge(raw_in, 16 * 9)
            for k in range(4):
                last = pe.transpose(p_a[:, k * P:(k + 1) * P], raw_lru[:, k * P:(k + 1) * P], ident[:, :])
            last.then_inc(pe_setup, 1)
            last = pe.transpose(p_b[:, GATE_AT:GATE_AT + E], raw_gate, ident[0:E, 0:E])
            for raw, at in ((raw_sg, SG_AT), (raw_su, SU_AT)):
                for c in range(SC):
                    last = pe.transpose(p_b[:, at + c * SH:at + (c + 1) * SH], raw[:, c, :], ident[0:SH, 0:SH])
            last.then_inc(pe_setup, 1)
            for c in range(SC):
                last = pe.transpose(p_c[0:SH, c * D:(c + 1) * D], raw_sd[:, c * SH:(c + 1) * SH], ident[:, :])
            last.then_inc(pe_setup, 1)

            def split(i):
                m, a = groups[i]
                q = next(q for q, (pm, pa, pe_) in enumerate(pieces) if pm == m and pa <= a < pe_)
                pe.wait_ge(stage_in[q % STAGES], loaded_at[q])
                if i >= 4:
                    pe.wait_ge(w_lo, i - 3)
                at = a - pieces[q][1]
                for c in range(GROUP):
                    last = pe.transpose(turn_banks[i % 4][:, c * P:(c + 1) * P],
                                        stage[q % STAGES][:, (at + c) * D:(at + c + 1) * D], ident[:, :])
                last.then_inc(w_turned, 1)

            def x_turn(n):
                after(pe, dve_step, DVE_STEPS, "xn", n)
                if first(n):
                    after(pe, dve_setup, DVE_SETUP, "lru_T")
                else:
                    after(pe, dve_step, DVE_STEPS, "turned_in", n - 1)
                for s in range(SUB):
                    last = pe.transpose(p_a[:, s * P:(s + 1) * P], x_in[:, s, :], ident[:, :])
                last.then_inc(pe_step, 1)

            def logits(n):
                after(pe, act_step, ACT_STEPS, "x_T", n)
                if first(n):
                    after(pe, dve_setup, DVE_SETUP, "shared_lo")
                else:
                    after(pe, dve_step, DVE_STEPS, "weight_T", n - 1)
                for s in range(SUB):
                    last = pe.matmul(p_b[:, s * E:(s + 1) * E], x_T[:, s * P:(s + 1) * P], gate_T[:, :],
                                     start=True, stop=True)
                last.then_inc(pe_step, 1)

            def drive(n):
                pe.matmul(p_a[:, :], lru_T[:, 0:P], x_T[:, :], start=True, stop=True)
                pe.matmul(p_c[:, :], lru_T[:, P:2 * P], x_T[:, :], start=True, stop=True).then_inc(pe_step, 1)

            def weight_turn(n):
                after(pe, dve_step, DVE_STEPS, "weight", n)
                for s in range(SUB):
                    last = pe.transpose(p_b[:, s * P:(s + 1) * P],
                                        weight[:, s, :, :].rearrange("p e r -> p (e r)"), ident[:, :])
                last.then_inc(pe_step, 1)

            def lru_out(n):
                after(pe, pool_step, POOL_STEPS, "state", n)
                if not first(n):
                    pe.wait_ge(y_moved, n)
                pe.matmul(p_y[:, :], lru_T[:, 2 * P:3 * P], h_re[:, :], start=True, stop=False)
                pe.matmul(p_y[:, :], lru_T[:, 3 * P:4 * P], h_im[:, :], start=False, stop=False).then_inc(pe_step, 1)

            def up(n, j):
                k, m = U * n + j, rows(j)
                if j == 0:
                    after(pe, act_step, ACT_STEPS, "x_hi", n)
                for bank, (w, s), ready in ((p_g[j % 2], (wg, sg), g_ready), (p_u[j % 2], (wu, su), u_ready)):
                    if j < J:
                        w_hi_, w_lo_ = (a[:, j * P:(j + 1) * P] for a in w)
                    else:
                        w_hi_, w_lo_ = (a[:, (j - J) * SH:(j - J + 1) * SH] for a in s)
                    if not (first(n) and j < 2):
                        if ready is g_ready:
                            pe.wait_ge(silu_ready, k - 1)
                        elif 2 <= j < J + 2:
                            pe.wait_ge(up_ready, J * n + j - 1)
                        else:
                            pe.wait_ge(hid_ready, k - 1)
                    pe.matmul(bank[0:m, :], w_hi_, x_hi[:, :], start=True, stop=False)
                    pe.matmul(bank[0:m, :], w_lo_, x_hi[:, :], start=False, stop=False)
                    if j == 0 and ready is g_ready:
                        after(pe, dve_step, DVE_STEPS, "x_lo", n)
                    pe.matmul(bank[0:m, :], w_hi_, x_lo[:, :], start=False, stop=True).then_inc(ready, 1)

            def down(n, j):
                k, m = U * n + j, rows(j)
                pe.wait_ge(lo_ready, k + 1)
                if j < J:
                    w_hi_, w_lo_ = (a[:, j * D:(j + 1) * D] for a in wd)
                else:
                    w_hi_, w_lo_ = (a[:, (j - J) * D:(j - J + 1) * D] for a in sd)
                h_hi_, h_lo_ = hid_hi[0:m, j % PARTS, :], hid_lo[0:m, j % PARTS, :]
                pe.matmul(p_y[:, :], w_hi_, h_hi_, start=False, stop=False)
                pe.matmul(p_y[:, :], w_lo_, h_hi_, start=False, stop=False)
                pe.matmul(p_y[:, :], w_hi_, h_lo_, start=False, stop=(j == U - 1)).then_inc(y_done, 1)

            def y_turn(n):
                pe.wait_ge(y_moved, n + 1)
                for s in range(SUB):
                    last = pe.transpose(p_c[:, s * P:(s + 1) * P], y_T[:, s * P:(s + 1) * P], ident[:, :])
                last.then_inc(y_turned, 1)

            for i in range(len(groups)):
                split(i)
            x_turn(0)
            logits(0)
            drive(0)
            weight_turn(0)
            pe.wait_ge(w_lo, N_PARTS)
            for j in range(HEAD):
                up(0, j)
                if j == LAG - 1:
                    lru_out(0)
                if j >= LAG:
                    down(0, j - LAG)
            prepare = {14: x_turn, 17: logits, 19: drive, 40: weight_turn}

            def rest(t, more):
                for j in range(HEAD, U):
                    up(t, j)
                    down(t, j - LAG)
                    if more and j in prepare:
                        prepare[j](t + 1)
                down(t, U - 3)

            with pe.Fori(0, NT - 1) as t:
                rest(t, True)
                up(t + 1, 0)
                down(t, U - 2)
                up(t + 1, 1)
                down(t, U - 1)
                up(t + 1, 2)
                lru_out(t + 1)
                up(t + 1, 3)
                down(t + 1, 0)
                up(t + 1, 4)
                down(t + 1, 1)
                y_turn(t)
            rest(NT - 1, False)
            down(NT - 1, U - 2)
            down(NT - 1, U - 1)
            y_turn(NT - 1)


_INS = ['L0_attn_inputs', 'L0_attn_nu_log', 'L0_attn_theta_log', 'L0_attn_B_re', 'L0_attn_B_im', 'L0_attn_C_re',
        'L0_attn_C_im', 'L0_attn_D_skip', 'L0_ffn_gate_w', 'L0_ffn_gate_bias', 'L0_ffn_Wg', 'L0_ffn_Wu', 'L0_ffn_Wd',
        'L0_ffn_Sg', 'L0_ffn_Su', 'L0_ffn_Sd']
_OUTS = [((16, 256, 128), 'float32')]


def kernel(**inputs):
    import numpy as _np
    import concourse.bacc as _bacc
    from concourse import mybir as _mybir
    from concourse.bass_utils import run_bass_kernel_spmd as _run

    nc = _bacc.Bacc("TRN2", target_bir_lowering=False, num_devices=1)
    arrays, args = {}, []
    for name in _INS:
        a = _np.ascontiguousarray(inputs[name])
        arrays[f"in_{name}_dram"] = a
        args.append(nc.dram_tensor(f"in_{name}_dram", a.shape, _mybir.dt.from_np(a.dtype), kind="ExternalInput").ap())
    for i, (shape, dtype) in enumerate(_OUTS):
        dt = _mybir.dt.from_np(_np.dtype(dtype))
        args.append(nc.dram_tensor(f"out_{i}_dram", shape, dt, kind="ExternalOutput").ap())
    build(nc, *args)
    r = _run(nc, [arrays], core_ids=[0])
    return r.results[0]["out_0_dram"]
```

```python
from contextlib import ExitStack

import concourse.bass as bass
from concourse import mybir

F32 = mybir.dt.float32
F32R = mybir.dt.float32r
ALU = mybir.AluOpType
ACT = mybir.ActivationFunctionType
AX = mybir.AxisListType

P = 128
PI = 3.14159265358979
TWO_PI_A = 6.28125
TWO_PI_B = 2 * PI - TWO_PI_A
ROUND = 12582912.0
GONE = -3.0e38
LN_EPS = 1e-05
LRU_EPS = 1e-05
WEIGHT_EPS = 1e-20
ROUTED_SCALE = 2.5
TOP_GROUPS = 4

DVE_STEPS = ["stats", "mean_var", "xn", "choice", "pair_max", "quad_max", "quad_second", "group_max", "group_second",
             "group_score", "beats", "ties", "order", "rank", "group_mask", "masked", "masked_zero", "top8", "struck",
             "chosen", "chosen_sum", "sum_eps", "sum_inv", "weight", "weight_T"]
DRIVE_STEPS = ["in_re_cos", "in_im_sin", "in_im_cos", "in_re_sin", "scan_re", "scan_im"]
ACT_STEPS = ["x_T", "scores"]
POOL_STEPS = ["var_eps", "rstd", "turned_re", "turned_im", "re_cos", "im_sin", "h_re", "re_sin", "im_cos", "state",
              "skip"]
PE_STEPS = ["x_turn", "logits", "drive_re", "drive_im", "weight_turn", "lru_out"]
POOL_SETUP = ["consts", "masks", "rates", "exponents", "powers", "one_e2", "one_e2_eps", "gamma"]
DVE_SETUP = ["angle", "turns", "whole_turns", "less_a", "less_b", "clamped", "size", "gate_T", "tables", "lru_T",
             "shared_lo"]
ACT_SETUP = ["sin_cos", "shared_hi"]
PE_SETUP = ["gate_turn", "lru_turn", "shared_turn", "down_turn"]


def after(eng, semaphore, steps, name, n=0):
    eng.wait_ge(semaphore, n * len(steps) + steps.index(name) + 1)


def build(nc, x, nu_log, theta_log, B_re, B_im, C_re, C_im, D_skip, gate_w, gate_bias,
          Wg, Wu, Wd, Sg, Su, Sd, out):
    BATCH, SEQ, D = x.shape
    E, I, _ = Wg.shape
    NG = 8
    PG = E // NG
    T = 512
    SUB = T // P
    NT = BATCH * SEQ // T
    NSEQ = T // SEQ
    R = P // E
    J = I // R
    SC = 2
    SH = Sg.shape[0] // SC
    U = J + SC
    LAG = 3
    HEAD = 5
    FIRST_STEP = 8
    BUF = 2
    RING = 4
    assert U % BUF == 0 and D == P and R * E == P and HEAD > LAG

    x_tiles = x.rearrange("b s d -> (b s) d").rearrange("(t s p) d -> t p s d", p=P, s=SUB)
    out_tiles = out.rearrange("b s d -> (b s) d").rearrange("(t s p) d -> t p s d", p=P, s=SUB)

    ctx = ExitStack()
    with ctx:
        def sb(name, shape, dt=F32):
            return ctx.enter_context(nc.sbuf_tensor(name, shape, dt))

        def pb(name):
            return ctx.enter_context(nc.psum_tensor(name, [P, 512], F32))

        def sem(name):
            return ctx.enter_context(nc.semaphore(name))

        with nc.sbuf_tensor("raw_wg", [P, J, D], F32) as raw_wg, nc.sbuf_tensor("raw_wu", [P, J, D], F32) as raw_wu, \
                nc.sbuf_tensor("raw_wd", [P, D, J], F32) as raw_wd:
            raw_w = (raw_wg, raw_wu)
        wg_lo, wu_lo = (sb(f"{w}_lo", [P, J * P], F32R) for w in ("wg", "wu"))
        work = sb("work", [P, (BUF + RING) * T])
        up_w = work[:, 0:BUF * T].rearrange("p (b t) -> p b t", b=BUF)
        hid = work[:, BUF * T:(BUF + RING) * T].rearrange("p (b t) -> p b t", b=RING)
        hid_hi = sb("hid_hi", [P, RING, T], F32R)
        hid_lo = sb("hid_lo", [P, RING, T], F32R)
        assert (BUF + 3 * RING) * T >= D * J
        wg = [sb("wg_hi", [P, J * P], F32R), wg_lo]
        wu = [sb("wu_hi", [P, J * P], F32R), wu_lo]
        wd = [sb(f"wd_{h}", [P, J * D], F32R) for h in ("hi", "lo")]
        sg = [sb(f"sg_{h}", [P, SC * SH], F32R) for h in ("hi", "lo")]
        su = [sb(f"su_{h}", [P, SC * SH], F32R) for h in ("hi", "lo")]
        sd = [sb(f"sd_{h}", [SH, SC * D], F32R) for h in ("hi", "lo")]
        gate_T = sb("gate_T", [P, E])
        lru_T = sb("lru_T", [P, 4 * P])
        bias = sb("bias", [P, E])
        ident = sb("ident", [P, P])
        before = sb("before", [P, NG, NG])
        cols = sb("cols", [P, 16])
        cos_t = sb("cos_t", [P, SEQ])
        sin_t = sb("sin_t", [P, SEQ])
        gcos_t = sb("gcos_t", [P, SEQ])
        gsin_t = sb("gsin_t", [P, SEQ])
        decay = sb("decay", [P, SEQ])
        minus_half = sb("minus_half", [P, SUB])
        eps = sb("eps", [P, SUB])
        x_in = sb("x_in", [P, SUB, D])
        x_res = sb("x_res", [P, SUB, D])
        x_T = sb("x_T", [P, T])
        x_hi = sb("x_hi", [P, T], F32R)
        x_lo = sb("x_lo", [P, T], F32R)
        weight_T = sb("weight_T", [P, T])
        skip = sb("skip", [P, T])
        h_re = sb("h_re", [P, T])
        h_im = sb("h_im", [P, T])
        lru = sb("lru", [P, 4, T])
        small = sb("small", [P, 64])
        route = sb("route", [P, 7 * SUB * E])
        stats = small[:, 0:24].rearrange("p (s k) -> p s k", k=6)
        mv = small[:, 24:32].rearrange("p (s k) -> p s k", k=2)
        var_eps, rstd, w_sum, w_sum_eps, w_inv = (small[:, 32 + SUB * k:32 + SUB * (k + 1)] for k in range(5))
        y_T = lru[:, 0, :]

        (NU_LOG, THETA_LOG, DSKIP, NU, THETA, NEG_NU, DECAY, NEG_2NU, E2, ONE_E2, ONE_E2_EPS, GAMMA, BASE_E,
         HALF, HALF_PI) = range(15)

        def col(k):
            return cols[:, k:k + 1]

        def part(k):
            return route[:, k * SUB * E:(k + 1) * SUB * E]

        NSG = SUB * NG
        scores, choice = part(0), part(1)
        hi4, lo4 = (part(2)[:, k * NSG * 4:(k + 1) * NSG * 4].rearrange("p (g k) -> p g k", k=4) for k in range(2))
        hi2, mid2, low2, second2 = (part(3)[:, k * NSG * 2:(k + 1) * NSG * 2].rearrange("p (g k) -> p g k", k=2)
                                    for k in range(4))
        best, mid1, low1, second, score, rank, group_mask = (part(4)[:, k * NSG:(k + 1) * NSG] for k in range(7))
        top8 = part(4)[:, 7 * NSG:8 * NSG].rearrange("p (s k) -> p s k", k=8)
        beats, ties = (part(k).rearrange("p (g h) -> p g h", h=NG) for k in (5, 6))
        masked, masked_zero, struck, chosen = part(5), part(6), part(5), part(6)
        weight = route[:, 2 * SUB * E:4 * SUB * E].rearrange("p (s e r) -> p s e r", s=SUB, r=R)

        p_g = [pb(f"p_g{i}") for i in range(2)]
        p_u = [pb(f"p_u{i}") for i in range(2)]
        p_y = pb("p_y")
        p_a = pb("p_a")
        p_b = pb("p_b")
        p_c = pb("p_c")

        raw_lru = skip[:, :]
        raw_gate = h_re[0:E, 0:D]
        raw_sd = h_re[:, D:D + SC * SH]
        raw_sg, raw_su = (h_im[0:SH, k * SC * D:(k + 1) * SC * D].rearrange("p (c d) -> p c d", c=SC)
                          for k in range(2))
        GROUP = 4
        groups = [(m, a) for a in range(0, J, GROUP) for m in range(2)]
        EARLY = 2
        turn_banks = [p_b, p_c]
        ROWS = 16
        pieces = range(0, D, ROWS)
        POOL_PIECES = len(pieces) - 1

        rates_in, gate_in, bias_in, lru_in, shared_in = (
            sem(s) for s in ("rates_in", "gate_in", "bias_in", "lru_in", "shared_in"))
        w_in = [sem(f"w_in{i}") for i in range(len(groups))]
        wd_in = [sem(f"wd_in{k}") for k in range(len(pieces))]
        x_loaded = sem("x_loaded")
        res_loaded = sem("res_loaded")
        stored = sem("stored")
        pool_setup, dve_setup, act_setup, pe_setup = (sem(f"{e}_setup") for e in ("pool", "dve", "act", "pe"))
        pool_step, dve_step, act_step, pe_step = (sem(f"{e}_step") for e in ("pool", "dve", "act", "pe"))
        dve_drive, x_hi_ready, x_lo_ready = sem("dve_drive"), sem("x_hi_ready"), sem("x_lo_ready")
        w_turned, w_hi, w_lo = sem("w_turned"), sem("w_hi"), sem("w_lo")
        wd_hi, wd_lo, wd_last = sem("wd_hi"), sem("wd_lo"), sem("wd_last")
        g_ready, u_ready, silu_ready, up_ready, hid_ready, hi_ready, lo_ready, y_done = (
            sem(s) for s in ("g_ready", "u_ready", "silu_ready", "up_ready", "hid_ready", "hi_ready", "lo_ready",
                             "y_done"))
        y_moved, y_turned, out_ready = sem("y_moved"), sem("y_turned"), sem("out_ready")

        def rows(j):
            return P if j < J else SH

        def ring_free(eng, semaphore, n, j):
            if j >= RING:
                eng.wait_ge(semaphore, U * n + j - RING + 1)
            elif not first(n):
                last = max(i for i in range(U) if i % RING == j)
                eng.wait_ge(semaphore, U * (n - 1) + last + 1)

        def first(n, tile=0):
            return isinstance(n, int) and n == tile

        def group_part(i, h):
            m, a = groups[i]
            return (wg, wu)[m][h][:, a * P:(a + GROUP) * P]

        def down_part(k, h):
            return wd[h][:, :].rearrange("p (j d) -> p d j", d=D)[:, pieces[k]:pieces[k] + ROWS, :]

        def raw_down(k):
            return raw_wd[:, pieces[k]:pieces[k] + ROWS, :]

        def turn_bank(i):
            return (p_g[0], p_u[0])[i] if i < EARLY else turn_banks[i % 2]

        turn_after = {j: i for j, i in enumerate(range(EARLY, 16))}
        turn_after.update({24 + 2 * k: i for k, i in enumerate(range(16, len(groups)))})

        block = ctx.enter_context(nc.Block())

        @block.sync
        def _(sp):
            for k, v in ((NU_LOG, nu_log), (THETA_LOG, theta_log)):
                sp.dma_start(col(k), v.rearrange("(p o) -> p o", o=1)).then_inc(rates_in, 16)
            sp.dma_start(x_in[:, :, :], x_tiles[0]).then_inc(x_loaded, 16)
            sp.dma_start(raw_gate, gate_w).then_inc(gate_in, 16)

            wide = [w.rearrange("e (r j) d -> (e r) j d", r=R) for w in (Wg, Wu)]

            def load_group(i):
                m, a = groups[i]
                sp.dma_start(raw_w[m][:, a:a + GROUP, :], wide[m][:, a:a + GROUP, :]).then_inc(w_in[i], 16)

            def load_down(k):
                d = pieces[k]
                for r in range(R):
                    sp.dma_start(raw_wd[r::R, d:d + ROWS, :],
                                 Wd[:, d:d + ROWS, r * J:(r + 1) * J]).then_inc(wd_in[k], 16)

            load_down(0)
            sp.dma_start(bias[:, :], gate_bias.partition_broadcast(P)).then_inc(bias_in, 16)
            load_group(0)
            load_group(1)
            load_down(1)
            for k, m in enumerate((B_re, B_im, C_re, C_im)):
                sp.dma_start(raw_lru[:, k * P:(k + 1) * P], m).then_inc(lru_in, 16)
            sp.dma_start(col(DSKIP), D_skip.rearrange("(p o) -> p o", o=1)).then_inc(lru_in, 16)
            load_down(2)
            sp.dma_start(raw_sg, Sg.rearrange("(c p) d -> p c d", c=SC)).then_inc(shared_in, 16)
            sp.dma_start(raw_su, Su.rearrange("(c p) d -> p c d", c=SC)).then_inc(shared_in, 16)
            sp.dma_start(raw_sd, Sd).then_inc(shared_in, 16)
            for k in range(3, len(pieces)):
                load_down(k)
            for i in range(EARLY, len(groups)):
                load_group(i)
            sp.dma_start(x_res[:, :, :], x_tiles[0]).then_inc(res_loaded, 16)

            def store(n):
                sp.wait_ge(out_ready, n + 1)
                sp.dma_start(out_tiles[n], x_res[:, :, :]).then_inc(stored, 16)

            with sp.Fori(0, NT - 1) as t:
                after(sp, pe_step, PE_STEPS, "x_turn", t)
                sp.dma_start(x_in[:, :, :], x_tiles[t + 1]).then_inc(x_loaded, 16)
                store(t)
                sp.wait_ge(stored, 16 * t + 16)
                sp.dma_start(x_res[:, :, :], x_tiles[t + 1]).then_inc(res_loaded, 16)
            store(NT - 1)
            sp.wait_ge(stored, 16 * NT)

        @block.gpsimd
        def _(pool):
            pool.memset(ident[:, :], 0.0)
            pool.memset(before[:, :, :], 1.0)
            pool.memset(minus_half[:, :], -0.5)
            pool.memset(eps[:, :], LN_EPS)
            pool.memset(col(BASE_E), 2.718281828459045)
            pool.memset(col(HALF), 0.5)
            pool.memset(col(HALF_PI), PI / 2)
            pool.iota(decay[:, :], [[1, SEQ]], base=0, channel_multiplier=0,
                      allow_small_or_imprecise_dtypes=True).then_inc(pool_setup, 1)
            after(pool, pool_setup, POOL_SETUP, "consts")
            pool.affine_select(out=ident[:, :], in_=ident[:, :], compare_op=ALU.not_equal, fill=1.0,
                               base=0, pattern=[[-1, P]], channel_multiplier=1)
            pool.affine_select(out=before[:, :, :], in_=before[:, :, :], compare_op=ALU.is_gt, fill=0.0,
                               base=0, pattern=[[1, NG], [-1, NG]], channel_multiplier=0).then_inc(pool_setup, 1)
            pool.wait_ge(rates_in, 32)
            pool.tensor_tensor(col(NU), col(BASE_E), col(NU_LOG), ALU.pow)
            pool.tensor_tensor(col(THETA), col(BASE_E), col(THETA_LOG), ALU.pow).then_inc(pool_setup, 1)
            after(pool, pool_setup, POOL_SETUP, "rates")
            pool.tensor_scalar(col(NEG_NU), col(NU), -1.0, None, ALU.mult)
            pool.tensor_scalar(col(NEG_2NU), col(NU), -2.0, None, ALU.mult).then_inc(pool_setup, 1)
            after(pool, pool_setup, POOL_SETUP, "exponents")
            pool.tensor_tensor(col(DECAY), col(BASE_E), col(NEG_NU), ALU.pow)
            pool.tensor_tensor(col(E2), col(BASE_E), col(NEG_2NU), ALU.pow).then_inc(pool_setup, 1)
            after(pool, pool_setup, POOL_SETUP, "powers")
            pool.tensor_scalar(col(ONE_E2), col(E2), -1.0, 1.0, ALU.mult, ALU.add).then_inc(pool_setup, 1)
            after(pool, pool_setup, POOL_SETUP, "one_e2")
            pool.tensor_scalar(col(ONE_E2_EPS), col(ONE_E2), LRU_EPS, None, ALU.add).then_inc(pool_setup, 1)
            after(pool, pool_setup, POOL_SETUP, "one_e2_eps")
            pool.tensor_tensor(col(GAMMA), col(ONE_E2_EPS), col(HALF), ALU.pow).then_inc(pool_setup, 1)

            def norm_scale(n):
                after(pool, dve_step, DVE_STEPS, "mean_var", n)
                pool.tensor_tensor(var_eps, mv[:, :, 1], eps[:, :], ALU.add).then_inc(pool_step, 1)
                after(pool, pool_step, POOL_STEPS, "var_eps", n)
                pool.tensor_tensor(rstd, var_eps, minus_half[:, :], ALU.pow).then_inc(pool_step, 1)

            def down_lo(k):
                pool.wait_ge(wd_hi, k + 1)
                pool.tensor_tensor(down_part(k, 1), raw_down(k),
                                   down_part(k, 0).bitcast(F32), ALU.subtract).then_inc(wd_lo, 1)

            def turned_re(n):
                after(pool, dve_drive, DRIVE_STEPS, "in_im_sin", n)
                pool.tensor_tensor(lru[:, 0, :], lru[:, 0, :], lru[:, 1, :], ALU.add).then_inc(pool_step, 1)

            def turned_im(n):
                after(pool, dve_drive, DRIVE_STEPS, "in_re_sin", n)
                pool.tensor_tensor(lru[:, 2, :], lru[:, 2, :], lru[:, 3, :], ALU.subtract).then_inc(pool_step, 1)

            def time(table):
                return table[:, :].unsqueeze(1).to_broadcast([P, NSEQ, SEQ])

            def by_time(a):
                return a.rearrange("p (s t) -> p s t", t=SEQ)

            def re_cos(n):
                after(pool, dve_drive, DRIVE_STEPS, "scan_re", n)
                if first(n):
                    after(pool, pe_setup, PE_SETUP, "down_turn")
                else:
                    after(pool, pe_step, PE_STEPS, "lru_out", n - 1)
                pool.tensor_tensor(by_time(h_re[:, :]), by_time(lru[:, 1, :]), time(cos_t), ALU.mult).then_inc(pool_step, 1)

            def im_sin(n):
                after(pool, dve_drive, DRIVE_STEPS, "scan_im", n)
                pool.tensor_tensor(by_time(lru[:, 0, :]), by_time(lru[:, 3, :]), time(sin_t), ALU.mult).then_inc(pool_step, 1)

            def real_state(n):
                after(pool, pool_step, POOL_STEPS, "im_sin", n)
                pool.tensor_tensor(h_re[:, :], h_re[:, :], lru[:, 0, :], ALU.subtract).then_inc(pool_step, 1)

            def re_sin(n):
                pool.tensor_tensor(by_time(h_im[:, :]), by_time(lru[:, 1, :]), time(sin_t), ALU.mult).then_inc(pool_step, 1)

            def im_cos(n):
                pool.tensor_tensor(by_time(lru[:, 2, :]), by_time(lru[:, 3, :]), time(cos_t), ALU.mult).then_inc(pool_step, 1)

            def state(n):
                after(pool, pool_step, POOL_STEPS, "im_cos", n)
                pool.tensor_tensor(h_im[:, :], h_im[:, :], lru[:, 2, :], ALU.add).then_inc(pool_step, 1)

            def skipped(n):
                after(pool, act_step, ACT_STEPS, "x_T", n)
                if first(n):
                    after(pool, pe_setup, PE_SETUP, "lru_turn")
                    pool.wait_ge(lru_in, 16 * 5)
                else:
                    pool.wait_ge(y_moved, n)
                pool.tensor_tensor(skip[:, :], x_T[:, :], col(DSKIP).to_broadcast([P, T]), ALU.mult).then_inc(pool_step, 1)

            def lo(n, j):
                k, m = U * n + j, rows(j)
                pool.wait_ge(hi_ready, k + 1)
                pool.tensor_tensor(hid_lo[0:m, j % RING, :], hid[0:m, j % RING, :],
                                   hid_hi[0:m, j % RING, :].bitcast(F32), ALU.subtract).then_inc(lo_ready, 1)

            prepare = {11: norm_scale, 23: turned_re, 25: turned_im, 29: re_cos, 31: im_sin, 33: real_state,
                       35: re_sin, 37: im_cos, 39: state}

            def head(n):
                for j in range(HEAD):
                    lo(n, j)
                    if j == 2:
                        skipped(n)

            norm_scale(0)
            for k in range(POOL_PIECES):
                down_lo(k)
            pool.wait_ge(wd_last, 1)
            recurrence = {0: turned_re, 1: turned_im, 4: re_cos, 5: im_sin, 6: real_state, 7: re_sin, 8: im_cos,
                          9: state, 10: skipped}
            for j in range(U):
                lo(0, j)
                if j in recurrence:
                    recurrence[j](0)
                if j in prepare:
                    prepare[j](1)
            head(1)
            with pool.Fori(1, NT - 1) as t:
                for j in range(HEAD, U):
                    lo(t, j)
                    if j in prepare:
                        prepare[j](t + 1)
                head(t + 1)
            for j in range(HEAD, U):
                lo(NT - 1, j)

        @block.scalar
        def _(act):
            after(act, dve_setup, DVE_SETUP, "size")
            act.activation(sin_t[:, :], lru[:, 2, 0:SEQ], ACT.Sin)
            act.activation(cos_t[:, :], lru[:, 3, 0:SEQ], ACT.Sin, scale=-1.0, bias=col(HALF_PI)).then_inc(act_setup, 1)

            def shared_high():
                after(act, pe_setup, PE_SETUP, "shared_turn")
                act.copy(sg[0][:, :], p_u[1][:, 0:SC * SH])
                act.copy(su[0][:, :], p_u[1][:, SC * SH:2 * SC * SH])
                after(act, pe_setup, PE_SETUP, "down_turn")
                act.copy(sd[0][:, :], p_y[0:SH, 0:SC * D]).then_inc(act_setup, 1)

            def x_transposed(n):
                after(act, pe_step, PE_STEPS, "x_turn", n)
                if not first(n):
                    after(act, pool_step, POOL_STEPS, "skip", n - 1)
                    act.wait_ge(x_lo_ready, n)
                act.copy(x_T[:, :], p_a[:, :]).then_inc(act_step, 1)

            def sigmoid(n):
                after(act, pe_step, PE_STEPS, "logits", n)
                if not first(n):
                    after(act, dve_step, DVE_STEPS, "chosen", n - 1)
                act.activation(scores, p_b[:, 0:SUB * E], ACT.Sigmoid).then_inc(act_step, 1)

            def x_high(n):
                after(act, act_step, ACT_STEPS, "x_T", n)
                if not first(n):
                    act.wait_ge(u_ready, U * n)
                act.copy(x_hi[:, :], x_T[:, :]).then_inc(x_hi_ready, 1)

            def silu(n, j):
                k, m = U * n + j, rows(j)
                act.wait_ge(g_ready, k + 1)
                act.activation(p_g[j % 2][0:m, :], p_g[j % 2][0:m, :], ACT.Silu).then_inc(silu_ready, 1)

            def hi(n, j):
                k, m = U * n + j, rows(j)
                act.wait_ge(hid_ready, k + 1)
                ring_free(act, y_done, n, j)
                act.copy(hid_hi[0:m, j % RING, :], hid[0:m, j % RING, :]).then_inc(hi_ready, 1)

            def group_hi(i):
                act.wait_ge(w_turned, i + 1)
                act.copy(group_part(i, 0), turn_bank(i)[:, :]).then_inc(w_hi, 1)

            def down_hi(k):
                act.wait_ge(wd_in[k], 16 * R)
                act.copy(down_part(k, 0), raw_down(k)).then_inc(wd_hi, 1)

            prepare = {16: x_transposed, 18: sigmoid}
            down_hi(0)
            x_transposed(0)
            x_high(0)
            sigmoid(0)
            group_hi(0)
            group_hi(1)
            down_hi(1)
            shared_high()
            for k in range(2, len(pieces)):
                down_hi(k)
            for j in range(HEAD):
                silu(0, j)
                if j == 1:
                    act.wait_ge(wd_lo, POOL_PIECES)
                    act.wait_ge(wd_last, 1)
                if j:
                    hi(0, j - 1)
                if j - 1 in turn_after:
                    group_hi(turn_after[j - 1])

            def rest(t, more):
                for j in range(HEAD, U):
                    silu(t, j)
                    if more and j == U - 1:
                        x_high(t + 1)
                    hi(t, j - 1)
                    if first(t) and j - 1 in turn_after:
                        group_hi(turn_after[j - 1])
                    if more and j in prepare:
                        prepare[j](t + 1)

            def head(t):
                silu(t + 1, 0)
                hi(t, U - 1)
                for j in range(1, HEAD):
                    silu(t + 1, j)
                    hi(t + 1, j - 1)

            rest(0, True)
            head(0)
            with act.Fori(1, NT - 1) as t:
                rest(t, True)
                head(t)
            rest(NT - 1, False)
            hi(NT - 1, U - 1)

        @block.vector
        def _(dve):
            setup_done = [0]

            def setup(ins):
                ins.then_inc(dve_setup, 1)
                setup_done[0] += 1
                dve.wait_ge(dve_setup, setup_done[0])

            def rotation():
                angle, turns, less = (lru[:, k, 0:SEQ] for k in range(3))
                size = lru[:, 3, 0:SEQ]
                after(dve, pool_setup, POOL_SETUP, "rates")
                setup(dve.tensor_scalar(angle, decay[:, :], col(THETA), None, ALU.mult))
                setup(dve.tensor_scalar(turns, angle, 1 / (2 * PI), ROUND, ALU.mult, ALU.add))
                setup(dve.tensor_scalar(turns, turns, ROUND, None, ALU.subtract))
                setup(dve.scalar_tensor_tensor(less, turns, -TWO_PI_A, angle, ALU.mult, ALU.add))
                setup(dve.scalar_tensor_tensor(less, turns, -TWO_PI_B, less, ALU.mult, ALU.add))
                setup(dve.tensor_scalar(less, less, 3.1415925, -3.1415925, ALU.min, ALU.max))
                setup(dve.scalar_tensor_tensor(size, less, -1.0, less, ALU.mult, ALU.max))

            def gate_in_place():
                after(dve, pe_setup, PE_SETUP, "gate_turn")
                setup(dve.tensor_copy(gate_T[:, :], p_c[:, 0:E]))

            def tables():
                after(dve, pool_setup, POOL_SETUP, "gamma")
                after(dve, act_setup, ACT_SETUP, "sin_cos")
                dve.tensor_scalar(gcos_t[:, :], cos_t[:, :], col(GAMMA), None, ALU.mult)
                dve.tensor_scalar(gsin_t[:, :], sin_t[:, :], col(GAMMA), None, ALU.mult)
                setup(dve.tensor_scalar(decay[:, :], decay[:, :], 0.0, col(DECAY), ALU.mult, ALU.add))

            def lru_in_place():
                after(dve, pe_setup, PE_SETUP, "lru_turn")
                dve.tensor_copy(lru_T[:, 0:3 * P], p_g[1][:, 0:3 * P])
                setup(dve.tensor_scalar(lru_T[:, 3 * P:4 * P], p_g[1][:, 3 * P:4 * P], -1.0, None, ALU.mult))

            def shared_low():
                after(dve, act_setup, ACT_SETUP, "shared_hi")
                dve.tensor_tensor(sg[1][:, :], p_u[1][:, 0:SC * SH], sg[0][:, :].bitcast(F32), ALU.subtract)
                dve.tensor_tensor(su[1][:, :], p_u[1][:, SC * SH:2 * SC * SH], su[0][:, :].bitcast(F32), ALU.subtract)
                setup(dve.tensor_tensor(sd[1][:, :], p_y[0:SH, 0:SC * D], sd[0][:, :].bitcast(F32), ALU.subtract))

            def group_lo(i):
                dve.wait_ge(w_hi, i + 1)
                dve.tensor_tensor(group_part(i, 1), turn_bank(i)[:, :], group_part(i, 0).bitcast(F32),
                                  ALU.subtract).then_inc(w_lo, 1)

            def down_lo(k):
                dve.wait_ge(wd_hi, k + 1)
                dve.tensor_tensor(down_part(k, 1), raw_down(k),
                                  down_part(k, 0).bitcast(F32), ALU.subtract).then_inc(wd_last, 1)

            def time(table):
                return table[:, :].unsqueeze(1).to_broadcast([P, NSEQ, SEQ])

            def by_time(a):
                return a.rearrange("p (s t) -> p s t", t=SEQ)

            def step(ins, name, n):
                ins.then_inc(dve_step, 1)
                after(dve, dve_step, DVE_STEPS, name, n)

            def norm_stats(n):
                dve.wait_ge(x_loaded, 16 * n + 16)
                for s in range(SUB):
                    last = dve.bn_stats(stats[:, s, :], x_in[:, s, :])
                last.then_inc(dve_step, 1)

            def norm_aggregate(n):
                if first(n):
                    after(dve, dve_step, DVE_STEPS, "stats", n)
                for s in range(SUB):
                    last = dve.bn_aggr(mv[:, s, :], stats[:, s, :])
                last.then_inc(dve_step, 1)

            def normalise(n):
                after(dve, pool_step, POOL_STEPS, "rstd", n)
                for s in range(SUB):
                    last = dve.tensor_scalar(x_in[:, s, :], x_in[:, s, :], mv[:, s, 0:1], rstd[:, s:s + 1],
                                             ALU.subtract, ALU.mult)
                last.then_inc(dve_step, 1)

            def in_re_cos(n):
                after(dve, pe_step, PE_STEPS, "drive_re", n)
                if first(n):
                    after(dve, act_setup, ACT_SETUP, "sin_cos")
                elif first(n, 1):
                    after(dve, pool_step, POOL_STEPS, "state", 0)
                dve.tensor_tensor(by_time(lru[:, 0, :]), by_time(p_a[:, :]), time(gcos_t), ALU.mult).then_inc(dve_drive, 1)

            def in_im_sin(n):
                after(dve, pe_step, PE_STEPS, "drive_im", n)
                dve.tensor_tensor(by_time(lru[:, 1, :]), by_time(p_c[:, :]), time(gsin_t), ALU.mult).then_inc(dve_drive, 1)

            def in_im_cos(n):
                dve.tensor_tensor(by_time(lru[:, 2, :]), by_time(p_c[:, :]), time(gcos_t), ALU.mult).then_inc(dve_drive, 1)

            def in_re_sin(n):
                dve.tensor_tensor(by_time(lru[:, 3, :]), by_time(p_a[:, :]), time(gsin_t), ALU.mult).then_inc(dve_drive, 1)

            def scan_re(n):
                after(dve, pool_step, POOL_STEPS, "turned_re", n)
                scan(0)

            def scan_im(n):
                after(dve, pool_step, POOL_STEPS, "turned_im", n)
                scan(2)

            def scan(k):
                for s in range(NSEQ):
                    at = slice(s * SEQ, (s + 1) * SEQ)
                    last = dve.tensor_tensor_scan(lru[:, k + 1, at], decay[:, :], lru[:, k, at], 0.0,
                                                  ALU.mult, ALU.add)
                last.then_inc(dve_drive, 1)

            def choice_scores(n):
                after(dve, act_step, ACT_STEPS, "scores", n)
                if first(n):
                    dve.wait_ge(bias_in, 16)
                step(dve.tensor_tensor(choice.rearrange("p (s e) -> p s e", e=E),
                                       scores.rearrange("p (s e) -> p s e", e=E),
                                       bias[:, :].unsqueeze(1).to_broadcast([P, SUB, E]), ALU.add), "choice", n)

            def group_pairs(n):
                c = choice.rearrange("p (g k) -> p g k", k=PG)
                dve.tensor_tensor(hi4, c[:, :, 0:4], c[:, :, 4:8], ALU.max)
                step(dve.tensor_tensor(lo4, c[:, :, 0:4], c[:, :, 4:8], ALU.min), "pair_max", n)

            def group_fours(n):
                dve.tensor_tensor(hi2, hi4[:, :, 0:2], hi4[:, :, 2:4], ALU.max)
                dve.tensor_tensor(mid2, hi4[:, :, 0:2], hi4[:, :, 2:4], ALU.min)
                step(dve.tensor_tensor(low2, lo4[:, :, 0:2], lo4[:, :, 2:4], ALU.max), "quad_max", n)
                step(dve.tensor_tensor(second2, mid2, low2, ALU.max), "quad_second", n)

            def group_scores(n):
                dve.tensor_tensor(best, hi2[:, :, 0], hi2[:, :, 1], ALU.max)
                dve.tensor_tensor(mid1, hi2[:, :, 0], hi2[:, :, 1], ALU.min)
                step(dve.tensor_tensor(low1, second2[:, :, 0], second2[:, :, 1], ALU.max), "group_max", n)
                step(dve.tensor_tensor(second, mid1, low1, ALU.max), "group_second", n)
                step(dve.tensor_tensor(score, best, second, ALU.add), "group_score", n)

            def group_rank(n):
                other = score.rearrange("p (s g) -> p s g", g=NG).unsqueeze(2).to_broadcast([P, SUB, NG, NG])
                own = score.rearrange("p (s g) -> p s g", g=NG).unsqueeze(3).to_broadcast([P, SUB, NG, NG])
                b4, t4 = (a.rearrange("p (s g) h -> p s g h", s=SUB) for a in (beats, ties))
                dve.tensor_tensor(b4, other, own, ALU.is_gt)
                step(dve.tensor_tensor(t4, other, own, ALU.is_equal), "beats", n)

            def group_ties(n):
                t3 = ties.rearrange("p (s g) h -> p s (g h)", s=SUB)
                prior = before[:, :, :].rearrange("p g h -> p (g h)").unsqueeze(1).to_broadcast([P, SUB, NG * NG])
                step(dve.tensor_tensor(t3, t3, prior, ALU.mult), "ties", n)

            def group_order(n):
                t3 = ties.rearrange("p (s g) h -> p s (g h)", s=SUB)
                b3 = beats.rearrange("p (s g) h -> p s (g h)", s=SUB)
                step(dve.tensor_tensor(b3, b3, t3, ALU.add), "order", n)
                step(dve.tensor_reduce(rank, beats, AX.X, ALU.add), "rank", n)

            def mask(n):
                step(dve.tensor_scalar(group_mask, rank, float(TOP_GROUPS), None, ALU.is_lt), "group_mask", n)
                step(dve.tensor_tensor(masked.rearrange("p (g k) -> p g k", k=PG),
                                       choice.rearrange("p (g k) -> p g k", k=PG),
                                       group_mask.unsqueeze(2).to_broadcast([P, NSG, PG]), ALU.mult), "masked", n)

            def mask_zero(n):
                step(dve.tensor_scalar(masked_zero, masked, 0.0, None, ALU.add), "masked_zero", n)

            def choose(n):
                for s in range(SUB):
                    last = dve.max(top8[:, s, :], masked_zero[:, s * E:(s + 1) * E])
                step(last, "top8", n)

            def strike(n):
                for s in range(SUB):
                    last = dve.match_replace(struck[:, s * E:(s + 1) * E], top8[:, s, :],
                                             masked_zero[:, s * E:(s + 1) * E], GONE)
                step(last, "struck", n)

            def chosen_scores(n):
                step(dve.scalar_tensor_tensor(chosen, struck, GONE / 2, scores, ALU.is_lt, ALU.mult), "chosen", n)

            def weigh(n):
                step(dve.tensor_reduce(w_sum, chosen.rearrange("p (s e) -> p s e", e=E), AX.X, ALU.add),
                     "chosen_sum", n)
                step(dve.tensor_scalar(w_sum_eps, w_sum, WEIGHT_EPS, None, ALU.add), "sum_eps", n)
                step(dve.reciprocal(w_inv, w_sum_eps), "sum_inv", n)

            def weights(n):
                if not first(n):
                    after(dve, pe_step, PE_STEPS, "weight_turn", n - 1)
                for s in range(SUB):
                    last = dve.tensor_scalar(weight[:, s, :, :],
                                             chosen[:, s * E:(s + 1) * E].unsqueeze(2).to_broadcast([P, E, R]),
                                             w_inv[:, s:s + 1], ROUTED_SCALE, ALU.mult, ALU.mult)
                last.then_inc(dve_step, 1)

            def weight_in(n):
                after(dve, pe_step, PE_STEPS, "weight_turn", n)
                dve.tensor_copy(weight_T[:, :], p_b[:, :]).then_inc(dve_step, 1)
                after(dve, dve_step, DVE_STEPS, "weight_T", n)

            def x_low(n):
                dve.wait_ge(x_hi_ready, n + 1)
                dve.tensor_tensor(x_lo[:, :], x_T[:, :], x_hi[:, :].bitcast(F32), ALU.subtract).then_inc(x_lo_ready, 1)

            def y_out(n):
                dve.wait_ge(y_done, U * n + U)
                after(dve, pool_step, POOL_STEPS, "skip", n)
                if not (isinstance(n, int) and n == NT - 1):
                    after(dve, pool_step, POOL_STEPS, "state", n + 1)
                dve.tensor_tensor(y_T, p_y[:, :], skip[:, :], ALU.add).then_inc(y_moved, 1)

            def add_x(n):
                dve.wait_ge(y_turned, n + 1)
                dve.wait_ge(res_loaded, 16 * n + 16)
                dve.tensor_tensor(x_res[:, :, :], p_c[:, :].rearrange("p (s d) -> p s d", s=SUB), x_res[:, :, :],
                                  ALU.add).then_inc(out_ready, 1)

            def unit(n, j, between=None):
                k, m = U * n + j, rows(j)
                dve.wait_ge(u_ready, k + 1)
                up = up_w[0:m, j % BUF, :]
                if j < J:
                    ins = dve.tensor_tensor(up, p_u[j % 2][0:m, :], weight_T[0:m, :], ALU.mult)
                else:
                    ins = dve.tensor_copy(up, p_u[j % 2][0:m, :])
                ins.then_inc(up_ready, 1)
                if between:
                    between(n + 1)
                dve.wait_ge(up_ready, k + 1)
                dve.wait_ge(silu_ready, k + 1)
                ring_free(dve, lo_ready, n, j)
                dve.tensor_tensor(hid[0:m, j % RING, :], p_g[j % 2][0:m, :], up_w[0:m, j % BUF, :],
                                  ALU.mult).then_inc(hid_ready, 1)

            prepare = {8: norm_stats, 10: norm_aggregate, 13: normalise, 20: in_re_cos, 21: in_im_sin, 22: in_im_cos,
                       23: in_re_sin, 24: choice_scores, 26: scan_re, 28: scan_im, 29: group_pairs, 30: group_fours,
                       31: group_scores, 32: group_rank, 33: group_ties, 34: group_order, 35: mask, 36: mask_zero,
                       37: choose, 38: strike, 39: chosen_scores, 40: weigh, 41: weights}

            norm_stats(0)
            norm_aggregate(0)
            rotation()
            normalise(0)
            gate_in_place()
            group_lo(0)
            x_low(0)
            choice_scores(0)
            group_pairs(0)
            group_lo(1)
            group_fours(0)
            group_scores(0)
            tables()
            group_rank(0)
            group_ties(0)
            lru_in_place()
            group_order(0)
            mask(0)
            mask_zero(0)
            shared_low()
            choose(0)
            strike(0)
            in_re_cos(0)
            in_im_sin(0)
            chosen_scores(0)
            weigh(0)
            weights(0)
            in_im_cos(0)
            in_re_sin(0)
            weight_in(0)
            down_lo(POOL_PIECES)
            dve.wait_ge(wd_lo, (BUF + RING) * T // (ROWS * J) + 1)
            scans = {3: scan_re, 5: scan_im}
            for j in range(HEAD):
                unit(0, j)
                if j in scans:
                    scans[j](0)
                if j - 1 in turn_after:
                    group_lo(turn_after[j - 1])

            def rest(t, more):
                for j in range(HEAD, U):
                    if more and prepare.get(j) is norm_aggregate:
                        after(dve, dve_step, DVE_STEPS, "stats", t + 1)
                    unit(t, j, x_low if more and j == U - 1 else None)
                    if first(t) and j in scans:
                        scans[j](0)
                    if first(t) and j - 1 in turn_after:
                        group_lo(turn_after[j - 1])
                    if more and j in prepare:
                        prepare[j](t + 1)
                    if more and j == J:
                        weight_in(t + 1)

            def head(t):
                for j in range(HEAD):
                    unit(t + 1, j)
                    if j == 1:
                        y_out(t)
                    if j == 4:
                        add_x(t)

            rest(0, True)
            head(0)
            with dve.Fori(1, NT - 1) as t:
                rest(t, True)
                head(t)
            rest(NT - 1, False)
            y_out(NT - 1)
            add_x(NT - 1)

        @block.tensor
        def _(pe):
            after(pe, pool_setup, POOL_SETUP, "masks")
            pe.wait_ge(gate_in, 16)
            pe.transpose(p_c[:, 0:E], raw_gate, ident[0:E, 0:E]).then_inc(pe_setup, 1)

            def lru_turn():
                pe.wait_ge(lru_in, 16 * 5)
                for k in range(4):
                    last = pe.transpose(p_g[1][:, k * P:(k + 1) * P], raw_lru[:, k * P:(k + 1) * P], ident[:, :])
                last.then_inc(pe_setup, 1)

            def shared_turn():
                pe.wait_ge(shared_in, 16 * 3)
                for k, raw in enumerate((raw_sg, raw_su)):
                    for c in range(SC):
                        at = (k * SC + c) * SH
                        last = pe.transpose(p_u[1][:, at:at + SH], raw[:, c, :], ident[0:SH, 0:SH])
                last.then_inc(pe_setup, 1)
                for c in range(SC):
                    last = pe.transpose(p_y[0:SH, c * D:(c + 1) * D], raw_sd[:, c * SH:(c + 1) * SH], ident[:, :])
                last.then_inc(pe_setup, 1)

            def group_turn(i):
                m, a = groups[i]
                pe.wait_ge(w_in[i], 16)
                if i >= EARLY:
                    if i < EARLY + 2:
                        if turn_bank(i) is p_b:
                            after(pe, dve_step, DVE_STEPS, "weight_T", 0)
                        else:
                            after(pe, dve_drive, DRIVE_STEPS, "in_im_cos", 0)
                    else:
                        pe.wait_ge(w_lo, i - 1)
                    if i >= 16:
                        after(pe, act_step, ACT_STEPS, "scores", 1)
                        after(pe, dve_drive, DRIVE_STEPS, "in_im_cos", 1)
                for c in range(GROUP):
                    last = pe.transpose(turn_bank(i)[:, c * P:(c + 1) * P],
                                        raw_w[m][:, a + c, :], ident[:, :])
                last.then_inc(w_turned, 1)

            def x_turn(n):
                after(pe, dve_step, DVE_STEPS, "xn", n)
                if not first(n):
                    after(pe, dve_drive, DRIVE_STEPS, "in_re_sin", n - 1)
                for s in range(SUB):
                    last = pe.transpose(p_a[:, s * P:(s + 1) * P], x_in[:, s, :], ident[:, :])
                last.then_inc(pe_step, 1)

            def logits(n):
                after(pe, act_step, ACT_STEPS, "x_T", n)
                if first(n):
                    after(pe, dve_setup, DVE_SETUP, "gate_T")
                elif first(n, 1):
                    pe.wait_ge(w_lo, 16)
                else:
                    after(pe, dve_step, DVE_STEPS, "weight_T", n - 1)
                for s in range(SUB):
                    last = pe.matmul(p_b[:, s * E:(s + 1) * E], x_T[:, s * P:(s + 1) * P], gate_T[:, :],
                                     start=True, stop=True)
                last.then_inc(pe_step, 1)

            def drive_re(n):
                if first(n):
                    after(pe, dve_setup, DVE_SETUP, "lru_T")
                pe.matmul(p_a[:, :], lru_T[:, 0:P], x_T[:, :], start=True, stop=True).then_inc(pe_step, 1)

            def drive_im(n):
                pe.matmul(p_c[:, :], lru_T[:, P:2 * P], x_T[:, :], start=True, stop=True).then_inc(pe_step, 1)

            def weight_turn(n):
                after(pe, dve_step, DVE_STEPS, "weight", n)
                if first(n, 1):
                    pe.wait_ge(w_lo, len(groups))
                for s in range(SUB):
                    last = pe.transpose(p_b[:, s * P:(s + 1) * P],
                                        weight[:, s, :, :].rearrange("p e r -> p (e r)"), ident[:, :])
                last.then_inc(pe_step, 1)

            def lru_out(n):
                after(pe, pool_step, POOL_STEPS, "state", n)
                pe.matmul(p_y[:, :], lru_T[:, 2 * P:3 * P], h_re[:, :], start=False, stop=False)
                pe.matmul(p_y[:, :], lru_T[:, 3 * P:4 * P], h_im[:, :], start=False, stop=False).then_inc(pe_step, 1)

            def up(n, j):
                k, m = U * n + j, rows(j)
                if j == 0:
                    pe.wait_ge(x_hi_ready, n + 1)
                if first(n) and j < J and j % GROUP == 0:
                    pe.wait_ge(w_lo, 2 * (j // GROUP + 1))
                if first(n) and j == 1:
                    after(pe, dve_setup, DVE_SETUP, "shared_lo")
                for bank, (w, s), ready in ((p_g[j % 2], (wg, sg), g_ready), (p_u[j % 2], (wu, su), u_ready)):
                    if j < J:
                        w_hi_, w_lo_ = (a[:, j * P:(j + 1) * P] for a in w)
                    else:
                        w_hi_, w_lo_ = (a[:, (j - J) * SH:(j - J + 1) * SH] for a in s)
                    if not (first(n) and j < 2):
                        pe.wait_ge(hid_ready if ready is g_ready else up_ready, k - 1)
                    pe.matmul(bank[0:m, :], w_lo_, x_hi[:, :], start=True, stop=False)
                    pe.matmul(bank[0:m, :], w_hi_, x_hi[:, :], start=False, stop=False)
                    if j == 0 and ready is g_ready:
                        pe.wait_ge(x_lo_ready, n + 1)
                    pe.matmul(bank[0:m, :], w_hi_, x_lo[:, :], start=False, stop=True).then_inc(ready, 1)

            def down(n, j):
                k, m = U * n + j, rows(j)
                pe.wait_ge(lo_ready, k + 1)
                if j == 0 and first(n):
                    pe.wait_ge(wd_lo, POOL_PIECES)
                    pe.wait_ge(wd_last, 1)
                if j == 0 and not first(n):
                    pe.wait_ge(y_moved, n)
                if j < J:
                    w_hi_, w_lo_ = (a[:, j * D:(j + 1) * D] for a in wd)
                else:
                    w_hi_, w_lo_ = (a[:, (j - J) * D:(j - J + 1) * D] for a in sd)
                h_hi_, h_lo_ = hid_hi[0:m, j % RING, :], hid_lo[0:m, j % RING, :]
                pe.matmul(p_y[:, :], w_lo_, h_hi_, start=(j == 0), stop=False)
                pe.matmul(p_y[:, :], w_hi_, h_hi_, start=False, stop=False)
                pe.matmul(p_y[:, :], w_hi_, h_lo_, start=False, stop=(j == U - 1)).then_inc(y_done, 1)

            def y_turn(n):
                pe.wait_ge(y_moved, n + 1)
                for s in range(SUB):
                    last = pe.transpose(p_c[:, s * P:(s + 1) * P], y_T[:, s * P:(s + 1) * P], ident[:, :])
                last.then_inc(y_turned, 1)

            prepare = {14: x_turn, 16: logits, 17: drive_re, 18: drive_im, 42: weight_turn}
            x_turn(0)
            logits(0)
            group_turn(0)
            group_turn(1)
            lru_turn()
            shared_turn()
            drive_re(0)
            drive_im(0)
            up(0, 0)
            up(0, 1)
            weight_turn(0)
            for j in range(HEAD):
                if j >= 2:
                    up(0, j)
                if j >= LAG:
                    down(0, j - LAG)
                if j in turn_after:
                    group_turn(turn_after[j])

            def rest(t, more):
                for j in range(HEAD, U):
                    up(t, j)
                    down(t, j - LAG)
                    if first(t) and j in turn_after:
                        group_turn(turn_after[j])
                    if first(t) and j == 13:
                        lru_out(0)
                    if more and j in prepare:
                        prepare[j](t + 1)
                down(t, U - 3)

            def head(t):
                up(t + 1, 0)
                down(t, U - 2)
                up(t + 1, 1)
                down(t, U - 1)
                up(t + 1, 2)
                up(t + 1, 3)
                down(t + 1, 0)
                up(t + 1, 4)
                down(t + 1, 1)
                y_turn(t)
                lru_out(t + 1)

            rest(0, True)
            head(0)
            with pe.Fori(1, NT - 1) as t:
                rest(t, True)
                head(t)
            rest(NT - 1, False)
            down(NT - 1, U - 2)
            down(NT - 1, U - 1)
            y_turn(NT - 1)


_INS = ['L0_attn_inputs', 'L0_attn_nu_log', 'L0_attn_theta_log', 'L0_attn_B_re', 'L0_attn_B_im', 'L0_attn_C_re',
        'L0_attn_C_im', 'L0_attn_D_skip', 'L0_ffn_gate_w', 'L0_ffn_gate_bias', 'L0_ffn_Wg', 'L0_ffn_Wu', 'L0_ffn_Wd',
        'L0_ffn_Sg', 'L0_ffn_Su', 'L0_ffn_Sd']
_OUTS = [((16, 256, 128), 'float32')]


def kernel(**inputs):
    import numpy as _np
    import concourse.bacc as _bacc
    from concourse import mybir as _mybir
    from concourse.bass_utils import run_bass_kernel_spmd as _run

    nc = _bacc.Bacc("TRN2", target_bir_lowering=False, num_devices=1)
    arrays, args = {}, []
    for name in _INS:
        a = _np.ascontiguousarray(inputs[name])
        arrays[f"in_{name}_dram"] = a
        args.append(nc.dram_tensor(f"in_{name}_dram", a.shape, _mybir.dt.from_np(a.dtype), kind="ExternalInput").ap())
    for i, (shape, dtype) in enumerate(_OUTS):
        dt = _mybir.dt.from_np(_np.dtype(dtype))
        args.append(nc.dram_tensor(f"out_{i}_dram", shape, dt, kind="ExternalOutput").ap())
    build(nc, *args)
    r = _run(nc, [arrays], core_ids=[0])
    return r.results[0]["out_0_dram"]
```

```python
from contextlib import ExitStack

import concourse.bass as bass
from concourse import mybir

F32 = mybir.dt.float32
F32R = mybir.dt.float32r
ALU = mybir.AluOpType
ACT = mybir.ActivationFunctionType
AX = mybir.AxisListType

P = 128
PI = 3.14159265358979
TWO_PI_A = 6.28125
TWO_PI_B = 2 * PI - TWO_PI_A
ROUND = 12582912.0
GONE = -3.0e38
LN_EPS = 1e-05
LRU_EPS = 1e-05
WEIGHT_EPS = 1e-20
ROUTED_SCALE = 2.5
TOP_GROUPS = 4

DVE_STEPS = ["stats", "mean_var", "xn", "choice", "pair_max", "quad_max", "quad_second", "group_max", "group_second",
             "group_score", "beats", "ties", "order", "rank", "group_mask", "masked", "masked_zero", "top8", "struck",
             "chosen", "chosen_sum", "sum_eps", "sum_inv", "weight", "weight_T"]
DRIVE_STEPS = ["in_im_sin", "in_im_cos", "in_re_cos", "in_re_sin", "scan_re", "scan_im"]
ACT_STEPS = ["x_T", "scores"]
NORM_STEPS = ["var_eps", "rstd"]
POOL_STEPS = ["skip", "turned_re", "turned_im", "re_cos", "im_sin", "h_re", "re_sin", "im_cos", "h_im"]
PE_STEPS = ["x_turn", "logits", "weight_turn"]
DRIVES = ["drive_im", "drive_re"]
POOL_SETUP = ["consts", "masks", "rates", "exponents", "powers", "one_e2", "one_e2_eps", "gamma"]
DVE_SETUP = ["gate_T", "angle", "turns", "whole_turns", "less_a", "less_b", "clamped", "size", "tables",
             "shared_lo", "lru_lo"]
ACT_SETUP = ["sin_cos", "lru_hi", "shared_hi"]
PE_SETUP = ["gate_turn", "lru_turn", "shared_turn", "down_turn"]


def after(eng, semaphore, steps, name, n=0):
    eng.wait_ge(semaphore, n * len(steps) + steps.index(name) + 1)


def build(nc, x, nu_log, theta_log, B_re, B_im, C_re, C_im, D_skip, gate_w, gate_bias,
          Wg, Wu, Wd, Sg, Su, Sd, out):
    BATCH, SEQ, D = x.shape
    E, I, _ = Wg.shape
    NG = 8
    PG = E // NG
    T = 512
    SUB = T // P
    NT = BATCH * SEQ // T
    NSEQ = T // SEQ
    R = P // E
    J = I // R
    SC = 2
    SH = Sg.shape[0] // SC
    U = J + SC
    LAG = 3
    HEAD = 5
    BUF = 2
    RING = 4
    LRU_AT = (36, 42)
    V = U + len(LRU_AT)
    assert U % BUF == 0 and V % RING == 0 and D == P and R * E == P and HEAD > LAG

    x_tiles = x.rearrange("b s d -> (b s) d").rearrange("(t s p) d -> t p s d", p=P, s=SUB)
    out_tiles = out.rearrange("b s d -> (b s) d").rearrange("(t s p) d -> t p s d", p=P, s=SUB)

    ctx = ExitStack()
    with ctx:
        def sb(name, shape, dt=F32):
            return ctx.enter_context(nc.sbuf_tensor(name, shape, dt))

        def pb(name):
            return ctx.enter_context(nc.psum_tensor(name, [P, 512], F32))

        def sem(name):
            return ctx.enter_context(nc.semaphore(name))

        with nc.sbuf_tensor("raw_wg", [P, J, D], F32) as raw_wg, nc.sbuf_tensor("raw_wu", [P, J, D], F32) as raw_wu, \
                nc.sbuf_tensor("raw_wd", [P, D, J], F32) as raw_wd:
            raw_w = (raw_wg, raw_wu)
        wg_lo, wu_lo = (sb(f"{w}_lo", [P, J * P], F32R) for w in ("wg", "wu"))
        work = sb("work", [P, (BUF + RING) * T])
        up_w = work[:, 0:BUF * T].rearrange("p (b t) -> p b t", b=BUF)
        hid = work[:, BUF * T:(BUF + RING) * T].rearrange("p (b t) -> p b t", b=RING)
        hid_hi = sb("hid_hi", [P, RING, T], F32R)
        hid_lo = sb("hid_lo", [P, RING, T], F32R)
        assert (BUF + 3 * RING) * T >= D * J
        wg = [sb("wg_hi", [P, J * P], F32R), wg_lo]
        wu = [sb("wu_hi", [P, J * P], F32R), wu_lo]
        wd = [sb(f"wd_{h}", [P, J * D], F32R) for h in ("hi", "lo")]
        sg = [sb(f"sg_{h}", [P, SC * SH], F32R) for h in ("hi", "lo")]
        su = [sb(f"su_{h}", [P, SC * SH], F32R) for h in ("hi", "lo")]
        sd = [sb(f"sd_{h}", [SH, SC * D], F32R) for h in ("hi", "lo")]
        gate_T = sb("gate_T", [P, E])
        lru_w = [sb(f"lru_{h}", [P, 4 * P], F32R) for h in ("hi", "lo")]
        bias = sb("bias", [P, E])
        ident = sb("ident", [P, P])
        before = sb("before", [P, NG, NG])
        cols = sb("cols", [P, 16])
        cos_t = sb("cos_t", [P, SEQ])
        sin_t = sb("sin_t", [P, SEQ])
        gcos_t = sb("gcos_t", [P, SEQ])
        gsin_t = sb("gsin_t", [P, SEQ])
        decay = sb("decay", [P, SEQ])
        minus_half = sb("minus_half", [P, SUB])
        eps = sb("eps", [P, SUB])
        x_in = sb("x_in", [P, SUB, D])
        x_res = sb("x_res", [P, SUB, D])
        x_T = sb("x_T", [P, T])
        x_hi = sb("x_hi", [P, T], F32R)
        x_lo = sb("x_lo", [P, T], F32R)
        weight_T = sb("weight_T", [P, T])
        skip = sb("skip", [P, T])
        lru = sb("lru", [P, 4, T])
        small = sb("small", [P, 64])
        route = sb("route", [P, 7 * SUB * E])
        stats = small[:, 0:24].rearrange("p (s k) -> p s k", k=6)
        mv = small[:, 24:32].rearrange("p (s k) -> p s k", k=2)
        var_eps, rstd, w_sum, w_sum_eps, w_inv = (small[:, 32 + SUB * k:32 + SUB * (k + 1)] for k in range(5))
        h_parts = (lru[:, 0, :], lru[:, 2, :])
        y_T = lru[:, 0, :]

        (NU_LOG, THETA_LOG, DSKIP, NU, THETA, NEG_NU, DECAY, NEG_2NU, E2, ONE_E2, ONE_E2_EPS, GAMMA, BASE_E,
         HALF, HALF_PI) = range(15)

        def col(k):
            return cols[:, k:k + 1]

        def part(k):
            return route[:, k * SUB * E:(k + 1) * SUB * E]

        NSG = SUB * NG
        scores, choice = part(0), part(1)
        hi4, lo4 = (part(2)[:, k * NSG * 4:(k + 1) * NSG * 4].rearrange("p (g k) -> p g k", k=4) for k in range(2))
        hi2, mid2, low2, second2 = (part(3)[:, k * NSG * 2:(k + 1) * NSG * 2].rearrange("p (g k) -> p g k", k=2)
                                    for k in range(4))
        best, mid1, low1, second, score, rank, group_mask = (part(4)[:, k * NSG:(k + 1) * NSG] for k in range(7))
        top8 = part(4)[:, 7 * NSG:8 * NSG].rearrange("p (s k) -> p s k", k=8)
        beats, ties = (part(k).rearrange("p (g h) -> p g h", h=NG) for k in (5, 6))
        masked, masked_zero, struck, chosen = part(5), part(6), part(5), part(6)
        weight = route[:, 2 * SUB * E:4 * SUB * E].rearrange("p (s e r) -> p s e r", s=SUB, r=R)

        p_g = [pb(f"p_g{i}") for i in range(2)]
        p_u = [pb(f"p_u{i}") for i in range(2)]
        p_y = pb("p_y")
        p_a = pb("p_a")
        p_b = pb("p_b")
        p_c = pb("p_c")

        raw_lru = skip[:, :]
        x_res_flat = x_res[:, :, :].rearrange("p s d -> p (s d)")
        raw_gate = x_res_flat[0:E, 0:D]
        raw_sd = x_res_flat[:, D:D + SC * SH]
        raw_sg, raw_su = (lru[0:SH, k, SEQ:SEQ + SC * D].rearrange("p (c d) -> p c d", c=SC) for k in range(2))
        GROUP = 4
        groups = [(m, a) for a in range(0, J, GROUP) for m in range(2)]
        EARLY = 2
        LATE = 16
        turn_banks = [p_b, p_c]
        ROWS = 16
        pieces = range(0, D, ROWS)

        rates_in, gate_in, bias_in, lru_in, shared_in = (
            sem(s) for s in ("rates_in", "gate_in", "bias_in", "lru_in", "shared_in"))
        w_in = [sem(f"w_in{i}") for i in range(len(groups))]
        wd_in = [sem(f"wd_in{k}") for k in range(len(pieces))]
        x_loaded = sem("x_loaded")
        res_loaded = sem("res_loaded")
        stored = sem("stored")
        pool_setup, dve_setup, act_setup, pe_setup = (sem(f"{e}_setup") for e in ("pool", "dve", "act", "pe"))
        pool_step, dve_step, act_step, pe_step = (sem(f"{e}_step") for e in ("pool", "dve", "act", "pe"))
        pool_norm, pe_drive, dve_drive, x_hi_ready, x_lo_ready = (
            sem(s) for s in ("pool_norm", "pe_drive", "dve_drive", "x_hi_ready", "x_lo_ready"))
        w_turned, w_hi, w_lo = sem("w_turned"), sem("w_hi"), sem("w_lo")
        wd_hi, wd_lo = sem("wd_hi"), sem("wd_lo")
        g_ready, u_ready, silu_ready, up_ready, hid_ready, hi_ready, lo_ready, y_done = (
            sem(s) for s in ("g_ready", "u_ready", "silu_ready", "up_ready", "hid_ready", "hi_ready", "lo_ready",
                             "y_done"))
        y_moved, y_turned, out_ready = sem("y_moved"), sem("y_turned"), sem("out_ready")
        last_lo = sem("last_lo")

        def rows(j):
            return P if j < J else SH

        def half(n, h):
            return slice(h * n // 2, (h + 1) * n // 2)

        def place(j):
            return j + sum(j >= at for at in LRU_AT)

        lru_place = [at + r for r, at in enumerate(LRU_AT)]
        lru_behind = {at - 1: r for r, at in enumerate(LRU_AT)}

        def ring_free(eng, semaphore, n, q):
            if not first(n) or q >= RING:
                eng.wait_ge(semaphore, V * n + q - RING + 1)

        def is_tile(n, tile):
            return isinstance(n, int) and n == tile

        def first(n):
            return is_tile(n, 0)

        def group_part(i, h):
            m, a = groups[i]
            return (wg, wu)[m][h][:, a * P:(a + GROUP) * P]

        def down_part(k, h):
            return wd[h][:, :].rearrange("p (j d) -> p d j", d=D)[:, pieces[k]:pieces[k] + ROWS, :]

        def raw_down(k):
            return raw_wd[:, pieces[k]:pieces[k] + ROWS, :]

        def turn_bank(i):
            return (p_g[0], p_u[0])[i] if i < EARLY else turn_banks[i % 2]

        turn_after = {j: i for j, i in enumerate(range(EARLY, LATE))}
        turn_after.update({24 + 2 * k: i for k, i in enumerate(range(LATE, len(groups)))})

        block = ctx.enter_context(nc.Block())

        @block.sync
        def _(sp):
            sp.dma_start(x_in[:, :, :], x_tiles[0]).then_inc(x_loaded, 16)
            for k, v in ((NU_LOG, nu_log), (THETA_LOG, theta_log)):
                sp.dma_start(col(k), v.rearrange("(p o) -> p o", o=1)).then_inc(rates_in, 16)
            sp.dma_start(raw_gate, gate_w).then_inc(gate_in, 16)

            wide = [w.rearrange("e (r j) d -> (e r) j d", r=R) for w in (Wg, Wu)]

            def load_group(i):
                m, a = groups[i]
                sp.dma_start(raw_w[m][:, a:a + GROUP, :], wide[m][:, a:a + GROUP, :]).then_inc(w_in[i], 16)

            def load_down(k):
                d = pieces[k]
                for r in range(R):
                    sp.dma_start(raw_wd[r::R, d:d + ROWS, :],
                                 Wd[:, d:d + ROWS, r * J:(r + 1) * J]).then_inc(wd_in[k], 16)

            load_down(0)
            sp.dma_start(bias[:, :], gate_bias.partition_broadcast(P)).then_inc(bias_in, 16)
            load_group(0)
            load_group(1)
            load_down(1)
            for k, m in enumerate((B_re, B_im, C_re, C_im)):
                sp.dma_start(raw_lru[:, k * P:(k + 1) * P], m).then_inc(lru_in, 16)
            sp.dma_start(col(DSKIP), D_skip.rearrange("(p o) -> p o", o=1)).then_inc(lru_in, 16)
            load_down(2)
            sp.dma_start(raw_sg, Sg.rearrange("(c p) d -> p c d", c=SC)).then_inc(shared_in, 16)
            sp.dma_start(raw_su, Su.rearrange("(c p) d -> p c d", c=SC)).then_inc(shared_in, 16)
            sp.dma_start(raw_sd, Sd).then_inc(shared_in, 16)
            for k in range(3, len(pieces)):
                load_down(k)
            for i in range(EARLY, len(groups)):
                load_group(i)
            after(sp, pe_setup, PE_SETUP, "down_turn")
            sp.dma_start(x_res[:, :, :], x_tiles[0]).then_inc(res_loaded, 16)

            def store(n):
                sp.wait_ge(out_ready, n + 1)
                sp.dma_start(out_tiles[n], x_res[:, :, :]).then_inc(stored, 16)

            def load_x(n):
                after(sp, pe_step, PE_STEPS, "x_turn", n - 1)
                sp.dma_start(x_in[:, :, :], x_tiles[n]).then_inc(x_loaded, 16)

            def store_and_load_res(n):
                store(n)
                sp.wait_ge(stored, 16 * n + 16)
                sp.dma_start(x_res[:, :, :], x_tiles[n + 1]).then_inc(res_loaded, 16)

            load_x(1)
            with sp.Fori(0, NT - 2) as t:
                load_x(t + 2)
                store_and_load_res(t)
            store_and_load_res(NT - 2)
            for h in range(2):
                sp.wait_ge(out_ready, NT + h)
                sp.dma_start(out_tiles[NT - 1][:, half(SUB, h), :], x_res[:, half(SUB, h), :]).then_inc(stored, 16)
            sp.wait_ge(stored, 16 * (NT + 1))

        @block.gpsimd
        def _(pool):
            pool.memset(ident[:, :], 0.0)
            pool.memset(before[:, :, :], 1.0)
            pool.memset(minus_half[:, :], -0.5)
            pool.memset(eps[:, :], LN_EPS)
            pool.memset(col(BASE_E), 2.718281828459045)
            pool.memset(col(HALF), 0.5)
            pool.memset(col(HALF_PI), PI / 2)
            pool.iota(decay[:, :], [[1, SEQ]], base=0, channel_multiplier=0,
                      allow_small_or_imprecise_dtypes=True).then_inc(pool_setup, 1)
            after(pool, pool_setup, POOL_SETUP, "consts")
            pool.affine_select(out=ident[:, :], in_=ident[:, :], compare_op=ALU.not_equal, fill=1.0,
                               base=0, pattern=[[-1, P]], channel_multiplier=1)
            pool.affine_select(out=before[:, :, :], in_=before[:, :, :], compare_op=ALU.is_gt, fill=0.0,
                               base=0, pattern=[[1, NG], [-1, NG]], channel_multiplier=0).then_inc(pool_setup, 1)
            pool.wait_ge(rates_in, 32)
            pool.tensor_tensor(col(NU), col(BASE_E), col(NU_LOG), ALU.pow)
            pool.tensor_tensor(col(THETA), col(BASE_E), col(THETA_LOG), ALU.pow).then_inc(pool_setup, 1)
            def norm_scale(n):
                after(pool, dve_step, DVE_STEPS, "mean_var", n)
                pool.tensor_tensor(var_eps, mv[:, :, 1], eps[:, :], ALU.add).then_inc(pool_norm, 1)
                after(pool, pool_norm, NORM_STEPS, "var_eps", n)
                pool.tensor_tensor(rstd, var_eps, minus_half[:, :], ALU.pow).then_inc(pool_norm, 1)

            norm_scale(0)
            after(pool, pool_setup, POOL_SETUP, "rates")
            pool.tensor_scalar(col(NEG_NU), col(NU), -1.0, None, ALU.mult)
            pool.tensor_scalar(col(NEG_2NU), col(NU), -2.0, None, ALU.mult).then_inc(pool_setup, 1)
            after(pool, pool_setup, POOL_SETUP, "exponents")
            pool.tensor_tensor(col(DECAY), col(BASE_E), col(NEG_NU), ALU.pow)
            pool.tensor_tensor(col(E2), col(BASE_E), col(NEG_2NU), ALU.pow).then_inc(pool_setup, 1)
            after(pool, pool_setup, POOL_SETUP, "powers")
            pool.tensor_scalar(col(ONE_E2), col(E2), -1.0, 1.0, ALU.mult, ALU.add).then_inc(pool_setup, 1)
            after(pool, pool_setup, POOL_SETUP, "one_e2")
            pool.tensor_scalar(col(ONE_E2_EPS), col(ONE_E2), LRU_EPS, None, ALU.add).then_inc(pool_setup, 1)
            after(pool, pool_setup, POOL_SETUP, "one_e2_eps")
            pool.tensor_tensor(col(GAMMA), col(ONE_E2_EPS), col(HALF), ALU.pow).then_inc(pool_setup, 1)

            def down_lo(k):
                pool.wait_ge(wd_hi, k + 1)
                pool.tensor_tensor(down_part(k, 1), raw_down(k),
                                   down_part(k, 0).bitcast(F32), ALU.subtract).then_inc(wd_lo, 1)

            def turned_re(n):
                after(pool, dve_drive, DRIVE_STEPS, "in_re_cos", n)
                pool.tensor_tensor(lru[:, 0, :], lru[:, 0, :], lru[:, 1, :], ALU.add).then_inc(pool_step, 1)

            def turned_im(n):
                after(pool, dve_drive, DRIVE_STEPS, "in_re_sin", n)
                pool.tensor_tensor(lru[:, 2, :], lru[:, 2, :], lru[:, 3, :], ALU.subtract).then_inc(pool_step, 1)

            def time(table):
                return table[:, :].unsqueeze(1).to_broadcast([P, NSEQ, SEQ])

            def by_time(a):
                return a.rearrange("p (s t) -> p s t", t=SEQ)

            def re_cos(n):
                after(pool, dve_drive, DRIVE_STEPS, "scan_re", n)
                pool.tensor_tensor(by_time(lru[:, 0, :]), by_time(lru[:, 1, :]),
                                   time(cos_t), ALU.mult).then_inc(pool_step, 1)

            def im_sin(n):
                after(pool, dve_drive, DRIVE_STEPS, "scan_im", n)
                pool.tensor_tensor(by_time(lru[:, 2, :]), by_time(lru[:, 3, :]),
                                   time(sin_t), ALU.mult).then_inc(pool_step, 1)

            def real_state(n):
                after(pool, pool_step, POOL_STEPS, "im_sin", n)
                pool.tensor_tensor(h_parts[0], lru[:, 0, :], lru[:, 2, :], ALU.subtract).then_inc(pool_step, 1)

            def re_sin(n):
                after(pool, pool_step, POOL_STEPS, "h_re", n)
                pool.tensor_tensor(by_time(lru[:, 2, :]), by_time(lru[:, 1, :]),
                                   time(sin_t), ALU.mult).then_inc(pool_step, 1)

            def im_cos(n):
                after(pool, pool_step, POOL_STEPS, "re_sin", n)
                pool.tensor_tensor(by_time(lru[:, 1, :]), by_time(lru[:, 3, :]),
                                   time(cos_t), ALU.mult).then_inc(pool_step, 1)

            def imaginary_state(n):
                after(pool, pool_step, POOL_STEPS, "im_cos", n)
                pool.tensor_tensor(h_parts[1], lru[:, 2, :], lru[:, 1, :], ALU.add).then_inc(pool_step, 1)

            def skipped(n):
                after(pool, act_step, ACT_STEPS, "x_T", n)
                if first(n):
                    after(pool, pe_setup, PE_SETUP, "lru_turn")
                    pool.wait_ge(lru_in, 16 * 5)
                else:
                    pool.wait_ge(y_moved, n)
                pool.tensor_tensor(skip[:, :], x_T[:, :], col(DSKIP).to_broadcast([P, T]),
                                   ALU.mult).then_inc(pool_step, 1)

            def lo(n, j):
                q, m = place(j), rows(j)
                if is_tile(n, NT - 1) and j == U - 1:
                    return
                pool.wait_ge(hi_ready, V * n + q + 1)
                pool.tensor_tensor(hid_lo[0:m, q % RING, :], hid[0:m, q % RING, :],
                                   hid_hi[0:m, q % RING, :].bitcast(F32), ALU.subtract).then_inc(lo_ready, 1)
                if j in lru_behind:
                    r = lru_behind[j]
                    q = lru_place[r]
                    pool.wait_ge(hi_ready, V * n + q + 1)
                    pool.tensor_tensor(hid_lo[:, q % RING, :], h_parts[r], hid_hi[:, q % RING, :].bitcast(F32),
                                       ALU.subtract).then_inc(lo_ready, 1)

            recurrence = {20: turned_re, 22: turned_im, 27: re_cos, 29: im_sin, 31: real_state, 33: re_sin,
                          35: im_cos, 37: imaginary_state}

            def head(n):
                for j in range(HEAD):
                    lo(n, j)
                    if j == 2:
                        skipped(n)

            def rest(n, more):
                for j in range(HEAD, U):
                    lo(n, j)
                    if more and j == 8:
                        norm_scale(n + 1)
                    if j in recurrence:
                        recurrence[j](n)

            for k in range(len(pieces)):
                down_lo(k)
            pool.wait_ge(wd_lo, len(pieces))
            head(0)
            rest(0, True)
            head(1)
            with pool.Fori(1, NT - 1) as t:
                rest(t, True)
                head(t + 1)
            rest(NT - 1, False)

        @block.scalar
        def _(act):
            act.preload_act_table(ACT.Sin)

            def sin_and_cos():
                after(act, dve_setup, DVE_SETUP, "size")
                act.activation(sin_t[:, :], lru[:, 2, 0:SEQ], ACT.Sin)
                act.activation(cos_t[:, :], lru[:, 3, 0:SEQ], ACT.Sin, scale=-1.0,
                               bias=col(HALF_PI)).then_inc(act_setup, 1)

            def lru_high():
                after(act, pe_setup, PE_SETUP, "lru_turn")
                act.copy(lru_w[0][:, 0:3 * P], p_a[:, 0:3 * P])
                act.activation(lru_w[0][:, 3 * P:4 * P], p_a[:, 3 * P:4 * P], ACT.Copy,
                               scale=-1.0).then_inc(act_setup, 1)

            def shared_high():
                after(act, pe_setup, PE_SETUP, "shared_turn")
                act.copy(sg[0][:, :], p_c[:, 0:SC * SH])
                act.copy(su[0][:, :], p_c[:, SC * SH:2 * SC * SH])
                after(act, pe_setup, PE_SETUP, "down_turn")
                act.copy(sd[0][:, :], p_y[0:SH, 0:SC * D]).then_inc(act_setup, 1)

            def x_transposed(n):
                after(act, pe_step, PE_STEPS, "x_turn", n)
                if not first(n):
                    after(act, pool_step, POOL_STEPS, "skip", n - 1)
                    act.wait_ge(x_lo_ready, n)
                act.copy(x_T[:, :], p_a[:, :]).then_inc(act_step, 1)

            def sigmoid(n):
                after(act, pe_step, PE_STEPS, "logits", n)
                if not first(n):
                    after(act, dve_step, DVE_STEPS, "chosen", n - 1)
                act.activation(scores, p_b[:, 0:SUB * E], ACT.Sigmoid).then_inc(act_step, 1)

            def x_high(n):
                after(act, act_step, ACT_STEPS, "x_T", n)
                if not first(n):
                    act.wait_ge(u_ready, U * n)
                act.copy(x_hi[:, :], x_T[:, :]).then_inc(x_hi_ready, 1)

            def silu(n, j):
                k, m = U * n + j, rows(j)
                act.wait_ge(g_ready, k + 1)
                act.activation(p_g[j % 2][0:m, :], p_g[j % 2][0:m, :], ACT.Silu).then_inc(silu_ready, 1)

            def hi(n, j):
                q, m = place(j), rows(j)
                act.wait_ge(hid_ready, U * n + j + 1)
                ring_free(act, y_done, n, q)
                act.copy(hid_hi[0:m, q % RING, :], hid[0:m, q % RING, :]).then_inc(hi_ready, 1)
                if j in lru_behind:
                    r = lru_behind[j]
                    q = lru_place[r]
                    after(act, pool_step, POOL_STEPS, ("h_re", "h_im")[r], n)
                    ring_free(act, y_done, n, q)
                    act.copy(hid_hi[:, q % RING, :], h_parts[r]).then_inc(hi_ready, 1)

            def group_hi(i):
                act.wait_ge(w_turned, i + 1)
                act.copy(group_part(i, 0), turn_bank(i)[:, :]).then_inc(w_hi, 1)

            def down_hi(k):
                act.wait_ge(wd_in[k], 16 * R)
                act.copy(down_part(k, 0), raw_down(k)).then_inc(wd_hi, 1)

            prepare = {14: x_transposed, 16: sigmoid}
            down_hi(0)
            x_transposed(0)
            x_high(0)
            sin_and_cos()
            sigmoid(0)
            down_hi(1)
            group_hi(0)
            group_hi(1)
            down_hi(2)
            lru_high()
            shared_high()
            down_hi(3)
            down_hi(4)
            act.preload_act_table(ACT.Silu)
            for k in range(5, len(pieces)):
                down_hi(k)
            for j in range(HEAD):
                silu(0, j)
                if j == 1:
                    act.wait_ge(wd_lo, (BUF + RING + 2) * T // (ROWS * J) + 1)
                if j == 3:
                    act.wait_ge(wd_lo, len(pieces))
                if j:
                    hi(0, j - 1)
                if j - 1 in turn_after:
                    group_hi(turn_after[j - 1])

            def rest(t, more):
                for j in range(HEAD, U):
                    silu(t, j)
                    if more and j == U - 1:
                        x_high(t + 1)
                    hi(t, j - 1)
                    if first(t) and j - 1 in turn_after:
                        group_hi(turn_after[j - 1])
                    if more and j in prepare:
                        prepare[j](t + 1)

            def head(t):
                silu(t + 1, 0)
                hi(t, U - 1)
                for j in range(1, HEAD):
                    silu(t + 1, j)
                    hi(t + 1, j - 1)

            rest(0, True)
            head(0)
            with act.Fori(1, NT - 1) as t:
                rest(t, True)
                head(t)
            rest(NT - 1, False)
            hi(NT - 1, U - 1)

        @block.vector
        def _(dve):
            setup_done = [0]

            def setup(ins):
                ins.then_inc(dve_setup, 1)
                setup_done[0] += 1
                dve.wait_ge(dve_setup, setup_done[0])

            def rotation():
                angle, turns, less = (lru[:, k, 0:SEQ] for k in range(3))
                size = lru[:, 3, 0:SEQ]
                after(dve, pool_setup, POOL_SETUP, "rates")
                setup(dve.tensor_scalar(angle, decay[:, :], col(THETA), None, ALU.mult))
                setup(dve.tensor_scalar(turns, angle, 1 / (2 * PI), ROUND, ALU.mult, ALU.add))
                setup(dve.tensor_scalar(turns, turns, ROUND, None, ALU.subtract))
                setup(dve.scalar_tensor_tensor(less, turns, -TWO_PI_A, angle, ALU.mult, ALU.add))
                setup(dve.scalar_tensor_tensor(less, turns, -TWO_PI_B, less, ALU.mult, ALU.add))
                setup(dve.tensor_scalar(less, less, 3.1415925, -3.1415925, ALU.min, ALU.max))
                setup(dve.scalar_tensor_tensor(size, less, -1.0, less, ALU.mult, ALU.max))

            def gate_in_place():
                after(dve, pe_setup, PE_SETUP, "gate_turn")
                setup(dve.tensor_copy(gate_T[:, :], p_c[:, 0:E]))

            def tables():
                after(dve, pool_setup, POOL_SETUP, "gamma")
                after(dve, act_setup, ACT_SETUP, "sin_cos")
                dve.tensor_scalar(gcos_t[:, :], cos_t[:, :], col(GAMMA), None, ALU.mult)
                dve.tensor_scalar(gsin_t[:, :], sin_t[:, :], col(GAMMA), None, ALU.mult)
                setup(dve.tensor_scalar(decay[:, :], decay[:, :], 0.0, col(DECAY), ALU.mult, ALU.add))

            def shared_low(n):
                after(dve, act_setup, ACT_SETUP, "shared_hi")
                dve.tensor_tensor(sg[1][:, :], p_c[:, 0:SC * SH], sg[0][:, :].bitcast(F32), ALU.subtract)
                dve.tensor_tensor(su[1][:, :], p_c[:, SC * SH:2 * SC * SH], su[0][:, :].bitcast(F32), ALU.subtract)
                dve.tensor_tensor(sd[1][:, :], p_y[0:SH, 0:SC * D], sd[0][:, :].bitcast(F32),
                                  ALU.subtract).then_inc(dve_setup, 1)

            def lru_low():
                after(dve, act_setup, ACT_SETUP, "lru_hi")
                hi_part, lo_part = lru_w
                dve.tensor_tensor(lo_part[:, 0:3 * P], p_a[:, 0:3 * P], hi_part[:, 0:3 * P].bitcast(F32), ALU.subtract)
                dve.scalar_tensor_tensor(lo_part[:, 3 * P:4 * P], p_a[:, 3 * P:4 * P], -1.0,
                                         hi_part[:, 3 * P:4 * P].bitcast(F32), ALU.mult,
                                         ALU.subtract).then_inc(dve_setup, 1)

            def group_lo(i):
                dve.wait_ge(w_hi, i + 1)
                dve.tensor_tensor(group_part(i, 1), turn_bank(i)[:, :], group_part(i, 0).bitcast(F32),
                                  ALU.subtract).then_inc(w_lo, 1)

            def time(table):
                return table[:, :].unsqueeze(1).to_broadcast([P, NSEQ, SEQ])

            def by_time(a):
                return a.rearrange("p (s t) -> p s t", t=SEQ)

            def done(name, n):
                after(dve, dve_step, DVE_STEPS, name, n)

            def norm_stats(n):
                dve.wait_ge(x_loaded, 16 * n + 16)
                for s in range(SUB):
                    last = dve.bn_stats(stats[:, s, :], x_in[:, s, :])
                last.then_inc(dve_step, 1)

            def norm_aggregate(n):
                for s in range(SUB):
                    last = dve.bn_aggr(mv[:, s, :], stats[:, s, :])
                last.then_inc(dve_step, 1)

            def normalise(n):
                after(dve, pool_norm, NORM_STEPS, "rstd", n)
                for s in range(SUB):
                    last = dve.tensor_scalar(x_in[:, s, :], x_in[:, s, :], mv[:, s, 0:1], rstd[:, s:s + 1],
                                             ALU.subtract, ALU.mult)
                last.then_inc(dve_step, 1)

            def in_re_cos(n):
                after(dve, pe_drive, DRIVES, "drive_re", n)
                dve.tensor_tensor(by_time(lru[:, 0, :]), by_time(p_a[:, :]),
                                  time(gcos_t), ALU.mult).then_inc(dve_drive, 1)

            def in_im_sin(n):
                after(dve, pe_drive, DRIVES, "drive_im", n)
                dve.tensor_tensor(by_time(lru[:, 1, :]), by_time(p_c[:, :]),
                                  time(gsin_t), ALU.mult).then_inc(dve_drive, 1)

            def in_im_cos(n):
                dve.tensor_tensor(by_time(lru[:, 2, :]), by_time(p_c[:, :]),
                                  time(gcos_t), ALU.mult).then_inc(dve_drive, 1)

            def in_re_sin(n):
                dve.tensor_tensor(by_time(lru[:, 3, :]), by_time(p_a[:, :]),
                                  time(gsin_t), ALU.mult).then_inc(dve_drive, 1)

            def scan_re(n):
                after(dve, pool_step, POOL_STEPS, "turned_re", n)
                scan(0)

            def scan_im(n):
                after(dve, pool_step, POOL_STEPS, "turned_im", n)
                scan(2)

            def scan(k):
                for s in range(NSEQ):
                    at = slice(s * SEQ, (s + 1) * SEQ)
                    last = dve.tensor_tensor_scan(lru[:, k + 1, at], decay[:, :], lru[:, k, at], 0.0,
                                                  ALU.mult, ALU.add)
                last.then_inc(dve_drive, 1)

            def choice_scores(n):
                after(dve, act_step, ACT_STEPS, "scores", n)
                if first(n):
                    dve.wait_ge(bias_in, 16)
                dve.tensor_tensor(choice.rearrange("p (s e) -> p s e", e=E),
                                  scores.rearrange("p (s e) -> p s e", e=E),
                                  bias[:, :].unsqueeze(1).to_broadcast([P, SUB, E]), ALU.add).then_inc(dve_step, 1)

            def pair_max(n):
                c = choice.rearrange("p (g k) -> p g k", k=PG)
                dve.tensor_tensor(hi4, c[:, :, 0:4], c[:, :, 4:8], ALU.max)
                dve.tensor_tensor(lo4, c[:, :, 0:4], c[:, :, 4:8], ALU.min).then_inc(dve_step, 1)

            def quad_max(n):
                dve.tensor_tensor(hi2, hi4[:, :, 0:2], hi4[:, :, 2:4], ALU.max)
                dve.tensor_tensor(mid2, hi4[:, :, 0:2], hi4[:, :, 2:4], ALU.min)
                dve.tensor_tensor(low2, lo4[:, :, 0:2], lo4[:, :, 2:4], ALU.max).then_inc(dve_step, 1)

            def quad_second(n):
                dve.tensor_tensor(second2, mid2, low2, ALU.max).then_inc(dve_step, 1)

            def group_max(n):
                dve.tensor_tensor(best, hi2[:, :, 0], hi2[:, :, 1], ALU.max)
                dve.tensor_tensor(mid1, hi2[:, :, 0], hi2[:, :, 1], ALU.min)
                dve.tensor_tensor(low1, second2[:, :, 0], second2[:, :, 1], ALU.max).then_inc(dve_step, 1)

            def group_second(n):
                dve.tensor_tensor(second, mid1, low1, ALU.max).then_inc(dve_step, 1)

            def group_score(n):
                dve.tensor_tensor(score, best, second, ALU.add).then_inc(dve_step, 1)

            def group_beats(n):
                other = score.rearrange("p (s g) -> p s g", g=NG).unsqueeze(2).to_broadcast([P, SUB, NG, NG])
                own = score.rearrange("p (s g) -> p s g", g=NG).unsqueeze(3).to_broadcast([P, SUB, NG, NG])
                b4, t4 = (a.rearrange("p (s g) h -> p s g h", s=SUB) for a in (beats, ties))
                dve.tensor_tensor(b4, other, own, ALU.is_gt)
                dve.tensor_tensor(t4, other, own, ALU.is_equal).then_inc(dve_step, 1)

            def group_ties(n):
                t3 = ties.rearrange("p (s g) h -> p s (g h)", s=SUB)
                prior = before[:, :, :].rearrange("p g h -> p (g h)").unsqueeze(1).to_broadcast([P, SUB, NG * NG])
                dve.tensor_tensor(t3, t3, prior, ALU.mult).then_inc(dve_step, 1)

            def group_order(n):
                t3 = ties.rearrange("p (s g) h -> p s (g h)", s=SUB)
                b3 = beats.rearrange("p (s g) h -> p s (g h)", s=SUB)
                dve.tensor_tensor(b3, b3, t3, ALU.add).then_inc(dve_step, 1)

            def group_rank(n):
                dve.tensor_reduce(rank, beats, AX.X, ALU.add).then_inc(dve_step, 1)

            def top_groups(n):
                dve.tensor_scalar(group_mask, rank, float(TOP_GROUPS), None, ALU.is_lt).then_inc(dve_step, 1)

            def mask(n):
                dve.tensor_tensor(masked.rearrange("p (g k) -> p g k", k=PG),
                                  choice.rearrange("p (g k) -> p g k", k=PG),
                                  group_mask.unsqueeze(2).to_broadcast([P, NSG, PG]), ALU.mult).then_inc(dve_step, 1)

            def mask_zero(n):
                dve.tensor_scalar(masked_zero, masked, 0.0, None, ALU.add).then_inc(dve_step, 1)

            def choose(n):
                for s in range(SUB):
                    last = dve.max(top8[:, s, :], masked_zero[:, s * E:(s + 1) * E])
                last.then_inc(dve_step, 1)

            def strike(n):
                for s in range(SUB):
                    last = dve.match_replace(struck[:, s * E:(s + 1) * E], top8[:, s, :],
                                             masked_zero[:, s * E:(s + 1) * E], GONE)
                last.then_inc(dve_step, 1)

            def chosen_scores(n):
                dve.scalar_tensor_tensor(chosen, struck, GONE / 2, scores, ALU.is_lt, ALU.mult).then_inc(dve_step, 1)

            def chosen_sum(n):
                dve.tensor_reduce(w_sum, chosen.rearrange("p (s e) -> p s e", e=E), AX.X, ALU.add).then_inc(dve_step, 1)

            def sum_eps(n):
                dve.tensor_scalar(w_sum_eps, w_sum, WEIGHT_EPS, None, ALU.add).then_inc(dve_step, 1)

            def sum_inv(n):
                dve.reciprocal(w_inv, w_sum_eps).then_inc(dve_step, 1)

            def weights(n):
                if not first(n):
                    after(dve, pe_step, PE_STEPS, "weight_turn", n - 1)
                for s in range(SUB):
                    last = dve.tensor_scalar(weight[:, s, :, :],
                                             chosen[:, s * E:(s + 1) * E].unsqueeze(2).to_broadcast([P, E, R]),
                                             w_inv[:, s:s + 1], ROUTED_SCALE, ALU.mult, ALU.mult)
                last.then_inc(dve_step, 1)

            def weight_in(n):
                after(dve, pe_step, PE_STEPS, "weight_turn", n)
                dve.tensor_copy(weight_T[:, :], p_b[:, :]).then_inc(dve_step, 1)

            def x_low(n):
                dve.wait_ge(x_hi_ready, n + 1)
                dve.tensor_tensor(x_lo[:, :], x_T[:, :], x_hi[:, :].bitcast(F32), ALU.subtract).then_inc(x_lo_ready, 1)

            def y_out(n):
                dve.wait_ge(y_done, V * n + V)
                after(dve, pool_step, POOL_STEPS, "skip", n)
                dve.tensor_tensor(y_T, p_y[:, :], skip[:, :], ALU.add).then_inc(y_moved, 1)

            def add_x(n):
                dve.wait_ge(y_turned, n + 1)
                dve.wait_ge(res_loaded, 16 * n + 16)
                dve.tensor_tensor(x_res[:, :, :], p_c[:, :].rearrange("p (s d) -> p s d", s=SUB), x_res[:, :, :],
                                  ALU.add).then_inc(out_ready, 1)

            between = {6: "stats", 7: "mean_var", 11: "xn", 22: "choice", 23: "pair_max", 24: "quad_max",
                       26: "quad_second", 28: "group_max", 29: "group_second", 30: "group_score",
                       31: "beats", 32: "ties", 33: "order", 34: "rank", 35: "group_mask", 36: "masked_zero",
                       37: "top8", 38: "struck", 39: "chosen", 40: "chosen_sum", 41: "sum_inv", 44: "weight_T",
                       45: "x_lo"}
            recurrence = {18: in_im_sin, 19: in_im_cos, 20: in_re_cos, 21: in_re_sin, 25: scan_re, 27: scan_im}
            behind = {35: "masked", 40: "sum_eps", 41: "weight"}
            routing = {"stats": norm_stats, "mean_var": norm_aggregate, "xn": normalise, "choice": choice_scores,
                       "pair_max": pair_max, "quad_max": quad_max, "quad_second": quad_second,
                       "group_max": group_max, "group_second": group_second, "group_score": group_score,
                       "beats": group_beats, "ties": group_ties, "order": group_order, "rank": group_rank,
                       "group_mask": top_groups, "masked": mask, "masked_zero": mask_zero, "top8": choose,
                       "struck": strike, "chosen": chosen_scores, "chosen_sum": chosen_sum, "sum_eps": sum_eps,
                       "sum_inv": sum_inv, "weight": weights, "weight_T": weight_in}

            def unit(n, j, more=False):
                k, m = U * n + j, rows(j)
                dve.wait_ge(u_ready, k + 1)
                up = up_w[0:m, j % BUF, :]
                if j < J:
                    ins = dve.tensor_tensor(up, p_u[j % 2][0:m, :], weight_T[0:m, :], ALU.mult)
                else:
                    ins = dve.tensor_copy(up, p_u[j % 2][0:m, :])
                ins.then_inc(up_ready, 1)
                if more and j - 1 in behind:
                    done(behind[j - 1], n + 1)
                step = between.get(j) if more else None
                if step == "x_lo":
                    x_low(n + 1)
                elif step:
                    routing[step](n + 1)
                if j in recurrence:
                    recurrence[j](n)
                dve.wait_ge(up_ready, k + 1)
                dve.wait_ge(silu_ready, k + 1)
                ring_free(dve, lo_ready, n, place(j))
                dve.tensor_tensor(hid[0:m, place(j) % RING, :], p_g[j % 2][0:m, :], up_w[0:m, j % BUF, :],
                                  ALU.mult).then_inc(hid_ready, 1)
                if step in routing:
                    done(step, n + 1)
                if more and j in behind:
                    routing[behind[j]](n + 1)

            def steps(*names, meanwhile=()):
                for name in names:
                    routing[name](0)
                    if name == names[-1]:
                        for f, arg in meanwhile:
                            f(arg)
                    done(name, 0)

            steps("stats", "mean_var", "xn")
            gate_in_place()
            rotation()
            tables()
            steps("choice", "pair_max", "quad_max", meanwhile=[(group_lo, 0)])
            steps("quad_second", "group_max", meanwhile=[(group_lo, 1)])
            steps("group_second", meanwhile=[(x_low, 0)])
            steps("group_score", "beats")
            steps("ties", "order", "rank", "group_mask", "masked", "masked_zero", "top8", "struck", "chosen",
                  "chosen_sum", "sum_eps", "sum_inv", "weight", meanwhile=[(shared_low, 0)])
            steps("weight_T")
            dve.wait_ge(wd_lo, (BUF + RING) * T // (ROWS * J) + 1)
            for j in range(HEAD):
                unit(0, j)
                if j == 0:
                    lru_low()
                if j - 1 in turn_after:
                    group_lo(turn_after[j - 1])

            def rest(t, more):
                for j in range(HEAD, U):
                    unit(t, j, more)
                    if first(t) and j - 1 in turn_after:
                        group_lo(turn_after[j - 1])

            def head(t):
                for j in range(HEAD):
                    unit(t + 1, j)
                    if j == 1:
                        y_out(t)
                    if j == 4:
                        add_x(t)

            rest(0, True)
            head(0)
            with dve.Fori(1, NT - 1) as t:
                rest(t, True)
                head(t)
            rest(NT - 1, False)
            q = place(U - 1) % RING
            dve.wait_ge(hi_ready, V * NT)
            dve.tensor_tensor(hid_lo[0:SH, q, :], hid[0:SH, q, :], hid_hi[0:SH, q, :].bitcast(F32),
                              ALU.subtract).then_inc(last_lo, 1)
            dve.wait_ge(y_done, V * NT)
            after(dve, pool_step, POOL_STEPS, "skip", NT - 1)
            for h in range(2):
                dve.tensor_tensor(y_T[:, half(T, h)], p_y[:, half(T, h)], skip[:, half(T, h)],
                                  ALU.add).then_inc(y_moved, 1)
            dve.wait_ge(res_loaded, 16 * NT)
            for h in range(2):
                dve.wait_ge(y_turned, NT + h)
                dve.tensor_tensor(x_res[:, half(SUB, h), :],
                                  (p_c, p_a)[h][:, 0:T // 2].rearrange("p (s d) -> p s d", s=SUB // 2),
                                  x_res[:, half(SUB, h), :], ALU.add).then_inc(out_ready, 1)

        @block.tensor
        def _(pe):
            after(pe, pool_setup, POOL_SETUP, "masks")
            pe.wait_ge(gate_in, 16)
            pe.transpose(p_c[:, 0:E], raw_gate, ident[0:E, 0:E]).then_inc(pe_setup, 1)

            def lru_turn():
                pe.wait_ge(lru_in, 16 * 5)
                for k in range(4):
                    last = pe.transpose(p_a[:, k * P:(k + 1) * P], raw_lru[:, k * P:(k + 1) * P], ident[:, :])
                last.then_inc(pe_setup, 1)

            def shared_turn():
                pe.wait_ge(shared_in, 16 * 3)
                for k, raw in enumerate((raw_sg, raw_su)):
                    for c in range(SC):
                        at = (k * SC + c) * SH
                        last = pe.transpose(p_c[:, at:at + SH], raw[:, c, :], ident[0:SH, 0:SH])
                last.then_inc(pe_setup, 1)
                for c in range(SC):
                    last = pe.transpose(p_y[0:SH, c * D:(c + 1) * D], raw_sd[:, c * SH:(c + 1) * SH], ident[:, :])
                last.then_inc(pe_setup, 1)

            def group_turn(i):
                m, a = groups[i]
                pe.wait_ge(w_in[i], 16)
                if i >= EARLY:
                    if i < EARLY + 2:
                        if turn_bank(i) is p_b:
                            after(pe, dve_step, DVE_STEPS, "weight_T", 0)
                        else:
                            after(pe, dve_setup, DVE_SETUP, "shared_lo")
                    else:
                        pe.wait_ge(w_lo, i - 1)
                    if i >= LATE:
                        after(pe, act_step, ACT_STEPS, "scores", 1)
                        after(pe, dve_drive, DRIVE_STEPS, "in_im_cos", 0)
                for c in range(GROUP):
                    last = pe.transpose(turn_bank(i)[:, c * P:(c + 1) * P],
                                        raw_w[m][:, a + c, :], ident[:, :])
                last.then_inc(w_turned, 1)

            def x_turn(n):
                after(pe, dve_step, DVE_STEPS, "xn", n)
                if is_tile(n, 1):
                    after(pe, dve_setup, DVE_SETUP, "lru_lo")
                elif not first(n):
                    after(pe, dve_drive, DRIVE_STEPS, "in_re_sin", n - 2)
                for s in range(SUB):
                    last = pe.transpose(p_a[:, s * P:(s + 1) * P], x_in[:, s, :], ident[:, :])
                last.then_inc(pe_step, 1)

            def logits(n):
                after(pe, act_step, ACT_STEPS, "x_T", n)
                if first(n):
                    after(pe, dve_setup, DVE_SETUP, "gate_T")
                elif is_tile(n, 1):
                    pe.wait_ge(w_lo, LATE)
                else:
                    after(pe, dve_step, DVE_STEPS, "weight_T", n - 1)
                for s in range(SUB):
                    last = pe.matmul(p_b[:, s * E:(s + 1) * E], x_T[:, s * P:(s + 1) * P], gate_T[:, :],
                                     start=True, stop=True)
                last.then_inc(pe_step, 1)

            def drive(n, k, bank):
                b_hi, b_lo = (w[:, k * P:(k + 1) * P] for w in lru_w)
                pe.matmul(bank[:, :], b_lo, x_hi[:, :], start=True, stop=False)
                pe.matmul(bank[:, :], b_hi, x_hi[:, :], start=False, stop=False)
                pe.matmul(bank[:, :], b_hi, x_lo[:, :], start=False, stop=True).then_inc(pe_drive, 1)

            def drive_im(n):
                if first(n):
                    pe.wait_ge(w_lo, LATE)
                else:
                    pe.wait_ge(out_ready, n)
                drive(n, 1, p_c)

            def drive_re(n):
                after(pe, act_step, ACT_STEPS, "x_T", n if is_tile(n, NT - 1) else n + 1)
                drive(n, 0, p_a)

            def weight_turn(n):
                after(pe, dve_step, DVE_STEPS, "weight", n)
                if is_tile(n, 1):
                    pe.wait_ge(w_lo, len(groups))
                for s in range(SUB):
                    last = pe.transpose(p_b[:, s * P:(s + 1) * P],
                                        weight[:, s, :, :].rearrange("p e r -> p (e r)"), ident[:, :])
                last.then_inc(pe_step, 1)

            def up(n, j):
                k, m = U * n + j, rows(j)
                if j == 0:
                    pe.wait_ge(x_hi_ready, n + 1)
                if first(n) and j < J and j % GROUP == 0:
                    pe.wait_ge(w_lo, 2 * (j // GROUP + 1))
                for bank, (w, s), ready in ((p_g[j % 2], (wg, sg), g_ready), (p_u[j % 2], (wu, su), u_ready)):
                    if j < J:
                        w_hi_, w_lo_ = (a[:, j * P:(j + 1) * P] for a in w)
                    else:
                        w_hi_, w_lo_ = (a[:, (j - J) * SH:(j - J + 1) * SH] for a in s)
                    if not (first(n) and j < 2):
                        pe.wait_ge(hid_ready if ready is g_ready else up_ready, k - 1)
                    pe.matmul(bank[0:m, :], w_lo_, x_hi[:, :], start=True, stop=False)
                    pe.matmul(bank[0:m, :], w_hi_, x_hi[:, :], start=False, stop=False)
                    if j == 0 and ready is g_ready:
                        pe.wait_ge(x_lo_ready, n + 1)
                    pe.matmul(bank[0:m, :], w_hi_, x_lo[:, :], start=False, stop=True).then_inc(ready, 1)

            def down(n, j):
                q, m = place(j), rows(j)
                if j == 0 and first(n):
                    pe.wait_ge(wd_lo, len(pieces))
                if j == 0 and not first(n):
                    pe.wait_ge(y_moved, n)
                if j < J:
                    weights = [a[:, j * D:(j + 1) * D] for a in wd]
                else:
                    weights = [a[:, (j - J) * D:(j - J + 1) * D] for a in sd]
                join(n, q, m, weights)
                if j in lru_behind:
                    r = lru_behind[j]
                    join(n, lru_place[r], P, [a[:, (2 + r) * P:(3 + r) * P] for a in lru_w])

            def join(n, q, m, weights):
                w_hi_, w_lo_ = weights
                h_hi_, h_lo_ = hid_hi[0:m, q % RING, :], hid_lo[0:m, q % RING, :]
                if is_tile(n, NT - 1) and q == V - 1:
                    pe.wait_ge(last_lo, 1)
                else:
                    pe.wait_ge(lo_ready, V * n + q + 1)
                pe.matmul(p_y[:, :], w_lo_, h_hi_, start=(q == 0), stop=False)
                pe.matmul(p_y[:, :], w_hi_, h_hi_, start=False, stop=False)
                pe.matmul(p_y[:, :], w_hi_, h_lo_, start=False, stop=(q == V - 1)).then_inc(y_done, 1)

            def y_turn(n):
                pe.wait_ge(y_moved, n + 1)
                for s in range(SUB):
                    last = pe.transpose(p_c[:, s * P:(s + 1) * P], y_T[:, s * P:(s + 1) * P], ident[:, :])
                last.then_inc(y_turned, 1)

            prepare = {13: x_turn, 15: logits, 43: weight_turn}
            recurrence = {16: drive_im, 17: drive_re}
            x_turn(0)
            logits(0)
            group_turn(0)
            group_turn(1)
            lru_turn()
            shared_turn()
            up(0, 0)
            up(0, 1)
            weight_turn(0)
            for j in range(HEAD):
                if j >= 2:
                    up(0, j)
                if j >= LAG:
                    down(0, j - LAG)
                if j in turn_after:
                    group_turn(turn_after[j])

            def rest(t, more):
                for j in range(HEAD, U):
                    up(t, j)
                    down(t, j - LAG)
                    if first(t) and j in turn_after:
                        group_turn(turn_after[j])
                    if more and j in prepare:
                        prepare[j](t + 1)
                    if j in recurrence:
                        recurrence[j](t)
                down(t, U - 3)

            def head(t):
                up(t + 1, 0)
                down(t, U - 2)
                up(t + 1, 1)
                down(t, U - 1)
                up(t + 1, 2)
                up(t + 1, 3)
                down(t + 1, 0)
                up(t + 1, 4)
                down(t + 1, 1)
                y_turn(t)

            rest(0, True)
            head(0)
            with pe.Fori(1, NT - 1) as t:
                rest(t, True)
                head(t)
            rest(NT - 1, False)
            down(NT - 1, U - 2)
            down(NT - 1, U - 1)
            for h in range(2):
                pe.wait_ge(y_moved, NT + h)
                for s in range(SUB // 2):
                    at = (h * SUB // 2 + s) * P
                    last = pe.transpose((p_c, p_a)[h][:, s * P:(s + 1) * P], y_T[:, at:at + P], ident[:, :])
                last.then_inc(y_turned, 1)


_INS = ['L0_attn_inputs', 'L0_attn_nu_log', 'L0_attn_theta_log', 'L0_attn_B_re', 'L0_attn_B_im', 'L0_attn_C_re',
        'L0_attn_C_im', 'L0_attn_D_skip', 'L0_ffn_gate_w', 'L0_ffn_gate_bias', 'L0_ffn_Wg', 'L0_ffn_Wu', 'L0_ffn_Wd',
        'L0_ffn_Sg', 'L0_ffn_Su', 'L0_ffn_Sd']
_OUTS = [((16, 256, 128), 'float32')]


def kernel(**inputs):
    import numpy as _np
    import concourse.bacc as _bacc
    from concourse import mybir as _mybir
    from concourse.bass_utils import run_bass_kernel_spmd as _run

    nc = _bacc.Bacc("TRN2", target_bir_lowering=False, num_devices=1)
    arrays, args = {}, []
    for name in _INS:
        a = _np.ascontiguousarray(inputs[name])
        arrays[f"in_{name}_dram"] = a
        args.append(nc.dram_tensor(f"in_{name}_dram", a.shape, _mybir.dt.from_np(a.dtype), kind="ExternalInput").ap())
    for i, (shape, dtype) in enumerate(_OUTS):
        dt = _mybir.dt.from_np(_np.dtype(dtype))
        args.append(nc.dram_tensor(f"out_{i}_dram", shape, dt, kind="ExternalOutput").ap())
    build(nc, *args)
    r = _run(nc, [arrays], core_ids=[0])
    return r.results[0]["out_0_dram"]
```
